# Optimizing a Trainium2 kernel written in Bass

```python
import numpy as np
import jax
import jax.numpy as jnp

def _softmax(x, axis=-1):
    return jax.nn.softmax(x, axis=axis)

def _gelu(x):
    return jax.nn.gelu(x, approximate=True)

def _silu(x):
    return jax.nn.silu(x)

def _sigmoid(x):
    return jax.nn.sigmoid(x)

def _layernorm(x, axis=-1, eps=1e-05):
    m = jnp.mean(x, axis=axis, keepdims=True)
    v = jnp.var(x, axis=axis, keepdims=True)
    return (x - m) / jnp.sqrt(v + eps)

def _scatter_add(tgt, idx, src, axis=0):
    return tgt.at[idx].add(src)

def _segment_sum(src, seg, n):
    return jax.ops.segment_sum(src, seg, n)
kernel_name = 'mk_rec_standalone_d1_rec_r8_3a41ec'

def setup_inputs(seed: int=0):
    np.random.seed(seed)
    _w = jnp.asarray

    def _rec_inputs():
        import jax
        import jax.numpy as jnp
        _rk = jax.random.key(seed)
        r_x = -0.000392918 + 0.999932 * jax.random.normal(jax.random.fold_in(_rk, 1), (512, 32, 128), jnp.float32)
        r_noise = 0.000227908 + 0.99994 * jax.random.normal(jax.random.fold_in(_rk, 2), (512, 32, 8), jnp.float32)
        return (r_x, r_noise)
    r_x, r_noise = _rec_inputs()

    def _L0_rec_setup():
        import jax, jax.numpy as jnp
        import numpy as np
        NEG_INF = -1e+30

        def _layer_norm(x, w, b, eps=1e-05):
            mu = jnp.mean(x, axis=-1, keepdims=True)
            var = jnp.mean(jnp.square(x - mu), axis=-1, keepdims=True)
            return (x - mu) * jax.lax.rsqrt(var + eps) * w + b
        key = jax.random.key(seed)
        ks = jax.random.split(key, 24)
        B, T, C = (512, 32, 128)
        H, hs = (4, 32)
        E, K = (8, 2)
        Hf = 4 * C
        s = 0.02
        inp = {'x': jax.random.normal(ks[0], (B, T, C), jnp.float32), 'noise': jax.random.normal(ks[1], (B, T, E), jnp.float32), 'ln1_w': jnp.ones((C,), jnp.float32), 'ln1_b': jnp.zeros((C,), jnp.float32), 'ln2_w': jnp.ones((C,), jnp.float32), 'ln2_b': jnp.zeros((C,), jnp.float32), 'Wq': s * jax.random.normal(ks[2], (H, C, hs), jnp.float32), 'Wk': s * jax.random.normal(ks[3], (H, C, hs), jnp.float32), 'Wv': s * jax.random.normal(ks[4], (H, C, hs), jnp.float32), 'Wo': s * jax.random.normal(ks[5], (C, C), jnp.float32), 'bo': jnp.zeros((C,), jnp.float32), 'Wr': s * jax.random.normal(ks[6], (C, E), jnp.float32), 'br': jnp.zeros((E,), jnp.float32), 'Wn': s * jax.random.normal(ks[7], (C, E), jnp.float32), 'bn': jnp.zeros((E,), jnp.float32), 'Wsk': s * jax.random.normal(ks[8], (C, 1), jnp.float32), 'bsk': jnp.zeros((1,), jnp.float32), 'W1': s * jax.random.normal(ks[9], (E, C, Hf), jnp.float32), 'b1': jnp.zeros((E, Hf), jnp.float32), 'W2': s * jax.random.normal(ks[10], (E, Hf, C), jnp.float32), 'b2': jnp.zeros((E, C), jnp.float32), 'top_k': K}
        return inp
    _L0_rec_all = _L0_rec_setup()
    _L0_rec_in = {k: v for k, v in _L0_rec_all.items() if k in ('ln1_w', 'ln1_b', 'ln2_w', 'ln2_b', 'Wq', 'Wk', 'Wv', 'Wo', 'bo', 'Wr', 'br', 'Wn', 'bn', 'Wsk', 'bsk', 'W1', 'b1', 'W2', 'b2')}
    del _L0_rec_all
    return {'r_x': r_x, 'r_noise': r_noise, 'L0_rec_ln1_w': _L0_rec_in['ln1_w'], 'L0_rec_ln1_b': _L0_rec_in['ln1_b'], 'L0_rec_ln2_w': _L0_rec_in['ln2_w'], 'L0_rec_ln2_b': _L0_rec_in['ln2_b'], 'L0_rec_Wq': _L0_rec_in['Wq'], 'L0_rec_Wk': _L0_rec_in['Wk'], 'L0_rec_Wv': _L0_rec_in['Wv'], 'L0_rec_Wo': _L0_rec_in['Wo'], 'L0_rec_bo': _L0_rec_in['bo'], 'L0_rec_Wr': _L0_rec_in['Wr'], 'L0_rec_br': _L0_rec_in['br'], 'L0_rec_Wn': _L0_rec_in['Wn'], 'L0_rec_bn': _L0_rec_in['bn'], 'L0_rec_Wsk': _L0_rec_in['Wsk'], 'L0_rec_bsk': _L0_rec_in['bsk'], 'L0_rec_W1': _L0_rec_in['W1'], 'L0_rec_b1': _L0_rec_in['b1'], 'L0_rec_W2': _L0_rec_in['W2'], 'L0_rec_b2': _L0_rec_in['b2']}

def reference(r_x, r_noise, L0_rec_ln1_w, L0_rec_ln1_b, L0_rec_ln2_w, L0_rec_ln2_b, L0_rec_Wq, L0_rec_Wk, L0_rec_Wv, L0_rec_Wo, L0_rec_bo, L0_rec_Wr, L0_rec_br, L0_rec_Wn, L0_rec_bn, L0_rec_Wsk, L0_rec_bsk, L0_rec_W1, L0_rec_b1, L0_rec_W2, L0_rec_b2):
    import jax
    import jax.numpy as jnp

    def _L0_rec_ref(x, noise, ln1_w, ln1_b, ln2_w, ln2_b, Wq, Wk, Wv, Wo, bo, Wr, br, Wn, bn, Wsk, bsk, W1, b1, W2, b2, top_k):
        import jax, jax.numpy as jnp
        import numpy as np
        NEG_INF = -1e+30

        def _layer_norm(x, w, b, eps=1e-05):
            mu = jnp.mean(x, axis=-1, keepdims=True)
            var = jnp.mean(jnp.square(x - mu), axis=-1, keepdims=True)
            return (x - mu) * jax.lax.rsqrt(var + eps) * w + b
        B, T, C = x.shape
        E = Wr.shape[-1]
        h = _layer_norm(x, ln1_w, ln1_b)
        q = jnp.einsum('btc,hcs->bhts', h, Wq)
        k = jnp.einsum('btc,hcs->bhts', h, Wk)
        v = jnp.einsum('btc,hcs->bhts', h, Wv)
        scale = float(C) ** (-0.5)
        wei = jnp.einsum('bhts,bhus->bhtu', q, k) * scale
        causal = jnp.tril(jnp.ones((T, T), bool))
        wei = jnp.where(causal, wei, NEG_INF)
        wei = jax.nn.softmax(wei, axis=-1)
        attn = jnp.einsum('bhtu,bhus->bhts', wei, v)
        attn = attn.transpose(0, 2, 1, 3).reshape(B, T, C)
        x = x + attn @ Wo + bo
        nx = _layer_norm(x, ln2_w, ln2_b)
        logits = nx @ Wr + br
        noise_logits = nx @ Wn + bn
        noisy = logits + noise * jax.nn.softplus(noise_logits)
        _, idx = jax.lax.top_k(noisy, top_k)
        topmask = jax.nn.one_hot(idx, E, dtype=bool).any(axis=-2)
        router_out = jax.nn.softmax(jnp.where(topmask, noisy, NEG_INF), axis=-1)
        skip_prob = jax.nn.sigmoid(nx @ Wsk + bsk)[..., 0]
        non_skip = skip_prob <= 0.5
        expert_out = jnp.zeros_like(nx)
        for e in range(E):
            fe = jax.nn.relu(nx @ W1[e] + b1[e]) @ W2[e] + b2[e]
            expert_out = expert_out + router_out[..., e:e + 1] * fe
        final = jnp.where(non_skip[..., None], x + expert_out, x)
        return final
    y = _L0_rec_ref(r_x, r_noise, L0_rec_ln1_w, L0_rec_ln1_b, L0_rec_ln2_w, L0_rec_ln2_b, L0_rec_Wq, L0_rec_Wk, L0_rec_Wv, L0_rec_Wo, L0_rec_bo, L0_rec_Wr, L0_rec_br, L0_rec_Wn, L0_rec_bn, L0_rec_Wsk, L0_rec_bsk, L0_rec_W1, L0_rec_b1, L0_rec_W2, L0_rec_b2, 2)
    return y

_drawn_inputs = setup_inputs


def setup_inputs(seed=0):
    import zlib

    import numpy as np

    out = dict(_drawn_inputs(seed))
    spreads = {'L0_rec_ln1_w': (1.0, 0.6),
     'L0_rec_ln1_b': (0.0, 0.8),
     'L0_rec_ln2_w': (1.0, 0.594),
     'L0_rec_ln2_b': (0.0, 0.517),
     'L0_rec_bo': (0.0, 0.1),
     'L0_rec_br': (0.0, 0.41),
     'L0_rec_bn': (0.0, 0.588),
     'L0_rec_b1': (0.0, 0.538),
     'L0_rec_b2': (0.0, 0.1)}
    factors = {'L0_rec_Wq': 8.0,
     'L0_rec_Wk': 8.0,
     'L0_rec_Wv': 2.706,
     'L0_rec_Wo': 2.752,
     'L0_rec_Wn': 3.513}
    for name, (base, spread) in spreads.items():
        noise = np.random.default_rng([zlib.crc32(name.encode()), seed]).standard_normal(out[name].shape)
        drawn = base * np.exp(spread * noise) if base else spread * noise
        out[name] = jnp.asarray(drawn.astype(out[name].dtype))
    for name, factor in factors.items():
        out[name] = (out[name] * factor).astype(out[name].dtype)
    return out
```

```python
from contextlib import ExitStack

import concourse.bass as bass
from concourse import mybir

ALU = mybir.AluOpType
ACT = mybir.ActivationFunctionType
AX = mybir.AxisListType
F32 = mybir.dt.float32
F32R = mybir.dt.float32r
BF16 = mybir.dt.bfloat16
U32 = mybir.dt.uint32

P = 128
EPS = 1e-5
NEG = -1e30


def wait(eng, sem, value):
    if not (isinstance(value, int) and value <= 0):
        eng.wait_ge(sem, value)


def build(nc, x, noise, ln1_w, ln1_b, ln2_w, ln2_b, Wq, Wk, Wv, Wo, bo, Wr, br, Wn, bn, Wsk, bsk,
          W1, b1, W2, b2, out):
    B, T, C = x.shape
    H, _, HS = Wq.shape
    E, _, HF = W1.shape
    K = 2
    N = B * T
    J = 4
    G = J * P
    NG = N // G
    NB = P // T
    CH = HF // P
    MG = K * N // G + E
    ER = N + G
    RW = 132
    LW = 96
    NL = 2 * E + 1
    FAR = 1 << 24
    SCALE = float(C) ** -0.5
    assert C == P and HS == 32 and T == 32 and H * HS == C and NG % 2 == 0 and MG % 2 == 0

    xt = x.rearrange("b t c -> (b t) c").rearrange("(n p) c -> p n c", p=P)
    noise_t = noise.rearrange("b t e -> (b t) e").rearrange("(n p) e -> p n e", p=P)
    out_t = out.rearrange("b t c -> (b t) c").rearrange("(n p) c -> p n c", p=P)
    rows = nc.dram_tensor("expert_rows", [E * ER + E * G, RW], F32, kind="Internal").ap()
    results = nc.dram_tensor("expert_results", [K * N, C], F32, kind="Internal").ap()
    results_t = results.rearrange("(k n p) c -> p k n c", k=K, p=P)
    wsplit = nc.dram_tensor("split_weights", [E * P, 4 * HF], F32, kind="Internal").ap()
    biases = nc.dram_tensor("biases", [E * P, CH + 1], F32, kind="Internal").ap()

    ctx = ExitStack()
    with ctx:
        def sb(name, shape, dt=F32):
            return ctx.enter_context(nc.sbuf_tensor(name, shape, dt))

        def sem(name):
            return ctx.enter_context(nc.semaphore(name))

        ident = sb("ident", [P, P])
        before = sb("before", [P, P], BF16)
        ones = sb("ones", [P, P], BF16)
        zeros = sb("zeros", [P, P])
        causal = sb("causal", [P, T])
        in_batch = sb("in_batch", [P, NB, T])
        expert_no = sb("expert_no", [P, E])
        wq = sb("wq", [C, H, HS])
        wk = sb("wk", [C, H, HS])
        wv = sb("wv", [C, H, HS])
        wo = sb("wo", [C, C])
        wrouter = sb("wrouter", [C, LW])
        brouter = sb("brouter", [P, NL])
        bo_row = sb("bo_row", [P, C])
        norm1 = sb("norm1", [C, 2])
        norm2 = sb("norm2", [C, 2])
        one = sb("one", [P, 1])
        xres = sb("xres", [P, N // P, C])
        noise_sb = sb("noise_sb", [P, N // P, E])
        gates = sb("gates", [P, N // P, K])
        fill = sb("fill", [P, E])
        stats = sb("stats", [P, 2, J, 6])
        moments = sb("moments", [P, 2, J, 2])
        var_eps = sb("var_eps", [P, 2, J])
        log_var = sb("log_var", [P, 2, J])
        rstd0 = sb("rstd0", [P, 2, J])
        newt_a = sb("newt_a", [P, 2, J])
        newt_b = sb("newt_b", [P, 2, J])
        rstd = sb("rstd", [P, 2, J])
        z1 = sb("z1", [P, 2, J, C])
        z2 = sb("z2", [P, 2, J, C])
        hT = sb("hT", [C, G])
        qT = sb("qT", [C, G])
        kT = sb("kT", [C, G])
        v_sb = sb("v_sb", [P, 2, J, C])
        sc = sb("sc", [P, H, J, T])
        sc_m = sb("sc_m", [P, H, J, T])
        smax = sb("smax", [P, H, J])
        probs = sb("probs", [P, H, J, T])
        psum_row = sb("psum_row", [P, H, J])
        prec = sb("prec", [P, H, J])
        pn = sb("pn", [P, H, J, T])
        pT = sb("pT", [P, 2, H, J, T])
        oT = sb("oT", [C, J, NB, T])
        nT = sb("nT", [C, G])
        logit = sb("logit", [P, J, NL])
        nabs = sb("nabs", [P, J, E])
        nexp = sb("nexp", [P, J, E])
        nlog = sb("nlog", [P, J, E])
        spl = sb("spl", [P, J, E])
        nsp = sb("nsp", [P, J, E])
        noisy = sb("noisy", [P, J, E])
        top = sb("top", [P, J, 8])
        top_i = sb("top_i", [P, J, 8], U32)
        top_f = sb("top_f", [P, K, J])
        hot = sb("hot", [P, K, J, E])
        hot_any = sb("hot_any", [P, J, E], BF16)
        gdiff = sb("gdiff", [P, J])
        gexp = sb("gexp", [P, J])
        gden = sb("gden", [P, J])
        gfirst = sb("gfirst", [P, J])
        gsecond = sb("gsecond", [P, J])
        keep = sb("keep", [P, J])
        rowno = sb("rowno", [P, J, E])
        rowhot = sb("rowhot", [P, K * J, E])
        rows_of = sb("rows_of", [P, 2, K * J], U32)
        token = sb("token", [P, K, J])
        pay = sb("pay", [P, 2, K, J, RW])
        blocks_of = sb("blocks_of", [P, E])
        over = sb("over", [P, E, NG])
        steps512 = sb("steps512", [P, NG])
        below = sb("below", [P, E, E])
        ends3 = sb("ends3", [P, E, E])
        ends = sb("ends", [P, E])
        block_no = sb("block_no", [P, MG])
        past = sb("past", [P, MG, E])
        jump = sb("jump", [P, E])
        past_jump = sb("past_jump", [P, MG, E])
        exp_f = sb("exp_f", [P, MG])
        row_f = sb("row_f", [P, MG])
        weights_at = sb("weights_at", [P, MG], U32)
        rows_at = sb("rows_at", [P, MG], U32)
        fill_u = sb("fill_u", [P, E], U32)
        region_no = sb("region_no", [P, E])
        count = sb("count", [P, E])
        row_part = sb("row_part", [P, MG])
        blank = sb("blank", [P, J, RW])
        wraw = sb("wraw", [P, 2 * HF])
        wcut = sb("wcut", [P, 4 * HF], F32R)
        bias_t = sb("bias_t", [P, E, CH + 1])
        wexp = sb("wexp", [P, 2, 4 * HF], F32R)
        bexp = sb("bexp", [P, 2, CH + 1])
        xg = sb("xg", [P, 2, J, RW])
        words = sb("words", [P, 2, J], U32)
        x32 = sb("x32", [C, G])
        xhi = sb("xhi", [C, 2, G], F32R)
        xlo = sb("xlo", [C, 2, G], F32R)
        h32 = sb("h32", [P, 2, G])
        hhi = sb("hhi", [P, CH, G], F32R)
        hlo = sb("hlo", [P, CH, G], F32R)
        yT = sb("yT", [C, G])
        yrow = sb("yrow", [P, 2, J, C])
        yin = pay[:, :, :, :, 0:C]
        half = z1
        fin = z2

        ps = ctx.enter_context(nc.psum_tensor("ps", [P, 8, 512], F32))

        s_x_in0 = sem("x_in0")
        s_x_in1 = sem("x_in1")
        s_consts_in = sem("consts_in")
        s_biases_in = sem("biases_in")
        s_ident_set = sem("ident_set")
        s_batch_mask = sem("batch_mask")
        s_causal_made = sem("causal_made")
        s_mask_set = sem("mask_set")
        s_pool_consts = sem("pool_consts")
        s_router_zeroed = sem("router_zeroed")
        s_noise_in = sem("noise_in")
        s_raw_in = sem("raw_in")
        s_cut_high = sem("cut_high")
        s_cut_low = sem("cut_low")
        s_cut_out = sem("cut_out")
        s_bias_out = sem("bias_out")
        s_blank_set = sem("blank_set")
        s_blank_word = sem("blank_word")
        s_blank_out = sem("blank_out")
        s_pay_zeroed = sem("pay_zeroed")
        s_norm1 = sem("norm1")
        s_norm1_log = sem("norm1_log")
        s_norm1_r0 = sem("norm1_r0")
        s_norm2 = sem("norm2")
        s_norm2_log = sem("norm2_log")
        s_norm2_r0 = sem("norm2_r0")
        s_z1T_made = sem("z1T_made")
        s_hT_made = sem("hT_made")
        s_q_made = sem("q_made")
        s_q_copied = sem("q_copied")
        s_k_made = sem("k_made")
        s_k_copied = sem("k_copied")
        s_v_made = sem("v_made")
        s_v_copied = sem("v_copied")
        s_s_made = sem("s_made")
        s_s_masked = sem("s_masked")
        s_s_max = sem("s_max")
        s_s_less = sem("s_less")
        s_exp_made = sem("exp_made")
        s_p_sum = sem("p_sum")
        s_p_inv = sem("p_inv")
        s_p_norm = sem("p_norm")
        s_pT_made = sem("pT_made")
        s_o_made = sem("o_made")
        s_oT_made = sem("oT_made")
        s_wo_made = sem("wo_made")
        s_x1_made = sem("x1_made")
        s_bo_added = sem("bo_added")
        s_z2T_made = sem("z2T_made")
        s_nT_made = sem("nT_made")
        s_logits_made = sem("logits_made")
        s_route = sem("route")
        s_noise_exp = sem("noise_exp")
        s_noise_log = sem("noise_log")
        s_gate_exp = sem("gate_exp")
        s_rank_made = sem("rank_made")
        s_pay_word = sem("pay_word")
        s_token_next = sem("token_next")
        s_pay_made = sem("pay_made")
        s_sent0 = sem("sent0")
        s_sent1 = sem("sent1")
        s_table = sem("table")
        s_pads_out = sem("pads_out")
        s_e_in0 = sem("e_in0")
        s_e_in1 = sem("e_in1")
        s_w_in0 = sem("w_in0")
        s_w_in1 = sem("w_in1")
        s_words_kept = sem("words_kept")
        s_xgT_made = sem("xgT_made")
        s_x32_made = sem("x32_made")
        s_x_hi = sem("x_hi")
        s_x_lo = sem("x_lo")
        s_h_made = sem("h_made")
        s_h32_made = sem("h32_made")
        s_h_hi = sem("h_hi")
        s_h_lo = sem("h_lo")
        s_y_made = sem("y_made")
        s_yT_made = sem("yT_made")
        s_yrow_made = sem("yrow_made")
        s_yrow_copied = sem("yrow_copied")
        s_res_out0 = sem("res_out0")
        s_res_out1 = sem("res_out1")
        s_f_in0 = sem("f_in0")
        s_f_in1 = sem("f_in1")
        s_f_half = sem("f_half")
        s_f_made = sem("f_made")
        s_f_out0 = sem("f_out0")
        s_f_out1 = sem("f_out1")
        norm_step, norm_log, norm_r0 = [s_norm1, s_norm2], [s_norm1_log, s_norm2_log], [s_norm1_r0, s_norm2_r0]
        x_in, sent, e_in, w_in = ([s_x_in0, s_x_in1], [s_sent0, s_sent1], [s_e_in0, s_e_in1],
                                 [s_w_in0, s_w_in1])
        res_out, f_in, f_out = [s_res_out0, s_res_out1], [s_f_in0, s_f_in1], [s_f_out0, s_f_out1]
        NORM = 7
        ROUTE = 21
        SENT = 16 * K * J
        CONSTS = 16 * 11
        TABLE = 13

        pay_u = pay[:].bitcast(U32)
        blank_u = blank[:].bitcast(U32)
        xg_u = xg[:].bitcast(U32)

        def pair(n, par, per):
            if isinstance(n, int):
                return (n // 2) * per
            return n * (per // 2) - par * (per // 2)

        def tiles(a, n):
            return a[:, bass.ds(n * J, J), :]

        def tile(a, n, j):
            return a[:, bass.ds(n * J + j, 1), :]

        def pipeline(eng, step):
            for t in range(-2, 5):
                step(t, t % 2)
            with eng.Fori(5, NG - 4, 2) as t:
                step(t, 1)
                step(t + 1, 0)
            for t in range(NG - 3, NG + 3):
                step(t, t % 2)

        def apart(eng, *waits):
            known = [(q, v if isinstance(v, int) else eng.to_reg(v)) for q, v in waits]
            if not all(isinstance(v, int) for _, v in known):
                eng.wait_ge(s_pool_consts, 1)
            for q, v in known:
                wait(eng, q, v)

        def live(n):
            return not isinstance(n, int) or 0 <= n < NG

        def upto(n):
            return min(n, NG) if isinstance(n, int) else n

        block = ctx.enter_context(nc.Block())

        @block.sync
        def _(sp):
            def load_x(n, par):
                apart(sp, (s_norm1, (n - 1) * NORM))
                sp.dma_start(tiles(xres, n), xt[:, bass.ds(n * J, J), :]).then_inc(x_in[par], 16)

            load_x(0, 0)
            load_x(1, 1)
            sp.dma_start(norm1[:, 0:1], ln1_w.unsqueeze(1)).then_inc(s_consts_in, 16)
            sp.dma_start(norm1[:, 1:2], ln1_b.unsqueeze(1)).then_inc(s_consts_in, 16)
            sp.dma_start(norm2[:, 0:1], ln2_w.unsqueeze(1)).then_inc(s_consts_in, 16)
            sp.dma_start(norm2[:, 1:2], ln2_b.unsqueeze(1)).then_inc(s_consts_in, 16)
            sp.dma_start(wq[:], Wq.rearrange("h c s -> c h s")).then_inc(s_consts_in, 16)
            sp.dma_start(wk[:], Wk.rearrange("h c s -> c h s")).then_inc(s_consts_in, 16)
            sp.dma_start(wv[:], Wv.rearrange("h c s -> c h s")).then_inc(s_consts_in, 16)
            sp.dma_start(wo[:], Wo).then_inc(s_consts_in, 16)
            sp.wait_ge(s_router_zeroed, 1)
            sp.dma_start(wrouter[:, 0:E], Wr).then_inc(s_consts_in, 16)
            sp.dma_start(wrouter[:, E:2 * E], Wn).then_inc(s_consts_in, 16)
            sp.dma_start(wrouter[:, 2 * E:NL], Wsk).then_inc(s_consts_in, 16)
            sp.dma_start(bo_row[:], bo.partition_broadcast(P)).then_inc(s_biases_in, 16)
            sp.dma_start(brouter[:, 0:E], br.partition_broadcast(P)).then_inc(s_biases_in, 16)
            sp.dma_start(brouter[:, E:2 * E], bn.partition_broadcast(P)).then_inc(s_biases_in, 16)
            sp.dma_start(brouter[:, 2 * E:NL], bsk.partition_broadcast(P)).then_inc(s_biases_in, 16)
            sp.dma_start(noise_sb[:], noise_t).then_inc(s_noise_in, 16)
            with sp.Fori(2, NG - 1, 2) as n:
                load_x(n, 0)
                load_x(n + 1, 1)

            with nc.allow_non_contiguous_dma(reason="a few KB of biases"):
                for e in range(E):
                    sp.dma_start(bias_t[:, e, 0:CH], b1[e].rearrange("(k p) -> p k", p=P)).then_inc(s_biases_in, 16)
                    sp.dma_start(bias_t[:, e, CH:CH + 1], b2[e].unsqueeze(1)).then_inc(s_biases_in, 16)
            sp.wait_ge(s_biases_in, 16 * (4 + 2 * E))
            sp.dma_start(biases.rearrange("(e p) k -> p e k", p=P), bias_t[:]).then_inc(s_bias_out, 16)

            sp.wait_ge(s_blank_word, 1)
            for e in range(E):
                sp.dma_start(rows[E * ER + e * G:E * ER + (e + 1) * G, :].rearrange("(p j) c -> p j c", j=J),
                             blank[:]).then_inc(s_blank_out, 16)
            sp.wait_ge(s_table, TABLE)
            for e in range(E):
                first = sp.value_load(fill_u[0:1, e:e + 1], min_val=0, max_val=E * ER - G)
                sp.dma_start(rows[bass.ds(first, G), :].rearrange("(p j) c -> p j c", j=J),
                             blank[:]).then_inc(s_pads_out, 16)

            sp.wait_ge(s_blank_out, 16 * E)
            sp.wait_ge(s_pads_out, 16 * E)
            sp.wait_ge(s_bias_out, 16)
            sp.wait_ge(s_cut_out, 16 * E)
            for q in sent:
                sp.wait_ge(q, SENT * NG // 2)

            def load_block(i, par):
                row = sp.value_load(rows_at[0:1, bass.ds(i, 1)], min_val=0, max_val=E * ER + (E - 1) * G)
                at = sp.value_load(weights_at[0:1, bass.ds(i, 1)], min_val=0, max_val=(E - 1) * P)
                apart(sp, (s_x32_made, i - 1),
                          (s_words_kept, i - 1))
                sp.dma_start(xg[:, par], rows[bass.ds(row, G), :].rearrange("(p j) c -> p j c", j=J)
                             ).then_inc(e_in[par], 16)
                apart(sp, (s_yT_made, i - 1))
                sp.dma_start(wexp[:, par].bitcast(F32), wsplit[bass.ds(at, P), :]).then_inc(w_in[par], 16)
                sp.dma_start(bexp[:, par], biases[bass.ds(at, P), :]).then_inc(w_in[par], 16)

            load_block(0, 0)
            load_block(1, 1)
            with sp.Fori(2, MG - 1, 2) as i:
                load_block(i, 0)
                load_block(i + 1, 1)

            for q in res_out:
                sp.wait_ge(q, 16 * J * MG // 2)

            def load_results(n, par):
                apart(sp, (s_f_made, n - 1))
                for k in range(K):
                    sp.dma_start(yin[:, par, k], results_t[:, k, bass.ds(n * J, J), :]).then_inc(f_in[par], 16)

            load_results(0, 0)
            load_results(1, 1)
            with sp.Fori(2, NG - 1, 2) as n:
                load_results(n, 0)
                load_results(n + 1, 1)

        @block.tensor
        def _(pe):
            def transposes(to, of, ready):
                for j in range(J):
                    m = nc.tensor.transpose(to[:, j * P:(j + 1) * P], of[:, j], ident[:])
                m.then_inc(ready, 1)

            def step(t, par):
                odd = 1 - par
                n = t
                if live(n):
                    apart(pe, (s_k_copied, n + 1),
                              (s_oT_made, n - 1))
                    for j in range(J):
                        for b in range(NB):
                            for h in range(H):
                                at = slice(j * P + b * T, j * P + (b + 1) * T)
                                m = nc.tensor.matmul(ps[b * T:(b + 1) * T, h, j * T:(j + 1) * T],
                                                     qT[h * HS:(h + 1) * HS, at], kT[h * HS:(h + 1) * HS, at],
                                                     start=True, stop=True,
                                                     tile_position=(h * HS, b * T))
                    m.then_inc(s_s_made, 1)
                n = t + 1
                if live(n):
                    pe.wait_ge(s_norm1, (n + 1) * NORM)
                    wait(pe, s_x1_made, n - 2)
                    transposes(ps[:, 4, :], z1[:, odd], s_z1T_made)
                n = t - 2
                if live(n):
                    pe.wait_ge(s_norm2, (n + 1) * NORM)
                    wait(pe, s_k_copied, upto(n + 3))
                    transposes(ps[:, 6, :], z2[:, par], s_z2T_made)
                n = t + 1
                if live(n):
                    pe.wait_ge(s_hT_made, n + 1)
                    nc.tensor.matmul(ps[:, 4, :], wq[:].rearrange("c h s -> c (h s)"), hT[:],
                                     start=True, stop=True).then_inc(s_q_made, 1)
                    wait(pe, s_nT_made, n - 2)
                    nc.tensor.matmul(ps[:, 6, :], wk[:].rearrange("c h s -> c (h s)"), hT[:],
                                     start=True, stop=True).then_inc(s_k_made, 1)
                n = t - 3
                if live(n):
                    pe.wait_ge(s_route, n * ROUTE + 10)
                    wait(pe, s_route, n * ROUTE)
                    for j in range(J):
                        rank = ps[:, 7, 384 + j * E:384 + (j + 1) * E]
                        nc.tensor.matmul(rank, before[:], hot_any[:, j, :], start=True, stop=(j == 0))
                        for i in range(j):
                            nc.tensor.matmul(rank, ones[:], hot_any[:, i, :], start=False, stop=(i == j - 1))
                    for j in range(J):
                        m = nc.tensor.matmul(ps[:, 7, 416:416 + E], ones[:], hot_any[:, j, :],
                                             start=(j == 0), stop=(j == J - 1))
                    m.then_inc(s_rank_made, 1)
                n = t - 1
                if live(n):
                    apart(pe, (s_pT_made, n + 1),
                              (s_s_masked, upto(n + 2)))
                    for j in range(J):
                        for h in range(H):
                            for b in range(NB):
                                m = nc.tensor.matmul(ps[h * HS:(h + 1) * HS, b, P + j * T:P + (j + 1) * T],
                                                     v_sb[b * T:(b + 1) * T, odd, j, h * HS:(h + 1) * HS],
                                                     pT[b * T:(b + 1) * T, odd, h, j, :], start=True, stop=True,
                                                     tile_position=(b * T, h * HS))
                    m.then_inc(s_o_made, 1)
                n = t + 1
                if live(n):
                    wait(pe, s_v_copied, n)
                    for j in range(J):
                        m = nc.tensor.matmul(ps[:, 5, j * P:(j + 1) * P], hT[:, j * P:(j + 1) * P],
                                             wv[:].rearrange("c h s -> c (h s)"), start=True, stop=True)
                    m.then_inc(s_v_made, 1)
                n = t - 1
                if live(n):
                    pe.wait_ge(s_oT_made, n + 1)
                    wait(pe, s_q_copied, upto(n + 3))
                    for j in range(J):
                        m = nc.tensor.matmul(ps[:, 4, j * P:(j + 1) * P], oT[:, j].rearrange("c b t -> c (b t)"),
                                             wo[:], start=True, stop=True)
                    m.then_inc(s_wo_made, 1)
                n = t - 2
                if live(n):
                    pe.wait_ge(s_nT_made, n + 1)
                    wait(pe, s_route, n * ROUTE)
                    for j in range(J):
                        m = nc.tensor.matmul(ps[:, 7, j * LW:(j + 1) * LW], nT[:, j * P:(j + 1) * P], wrouter[:],
                                             start=True, stop=True)
                    m.then_inc(s_logits_made, 1)

            pe.wait_ge(s_pool_consts, 1)
            pe.wait_ge(s_consts_in, CONSTS)
            pipeline(nc.tensor, step)

            def rows_in(i, par):
                pe.wait_ge(e_in[par], pair(i, par, 16) + 16)
                wait(pe, s_x32_made, i)
                transposes(ps[:, 5, :], xg[:, par, :, 0:C], s_xgT_made)

            def rows_out(i):
                wait(pe, s_yT_made, i + 1)
                wait(pe, s_yrow_copied, i)
                transposes(ps[:, 6, :], yT[:].rearrange("c (j p) -> c j p", j=J), s_yrow_made)

            def experts(i, par, first=False, last=False):
                pe.wait_ge(s_x_lo, i + 1)
                pe.wait_ge(w_in[par], pair(i, par, 32) + 32)
                for c in range(CH):
                    w_hi = wexp[:, par, c * P:(c + 1) * P]
                    w_lo = wexp[:, par, 2 * HF + c * P:2 * HF + (c + 1) * P]
                    wait(pe, s_h32_made, (i - 1) * CH + c + 1)
                    nc.tensor.matmul(ps[:, c, :], w_hi, xhi[:, par], start=True, stop=False)
                    nc.tensor.matmul(ps[:, c, :], w_hi, xlo[:, par], start=False, stop=False)
                    nc.tensor.matmul(ps[:, c, :], w_lo, xhi[:, par], start=False, stop=True).then_inc(s_h_made, 1)
                if not last:
                    rows_in(i + 1, 1 - par)
                if not first:
                    rows_out(i - 1)
                wait(pe, s_yT_made, i)
                for c in range(CH):
                    w_hi = wexp[:, par, HF + c * P:HF + (c + 1) * P]
                    w_lo = wexp[:, par, 3 * HF + c * P:3 * HF + (c + 1) * P]
                    pe.wait_ge(s_h_lo, i * CH + c + 1)
                    nc.tensor.matmul(ps[:, 4, :], w_hi, hhi[:, c], start=(c == 0), stop=False)
                    nc.tensor.matmul(ps[:, 4, :], w_lo, hhi[:, c], start=False, stop=False)
                    m = nc.tensor.matmul(ps[:, 4, :], w_hi, hlo[:, c], start=False, stop=(c == CH - 1))
                m.then_inc(s_y_made, 1)

            pe.wait_ge(s_route, NG * ROUTE)
            pe.wait_ge(s_x1_made, NG)
            pe.wait_ge(s_nT_made, NG)
            rows_in(0, 0)
            experts(0, 0, first=True)
            experts(1, 1)
            experts(2, 0)
            with nc.tensor.Fori(3, MG - 2, 2) as i:
                experts(i, 1)
                experts(i + 1, 0)
            experts(MG - 1, 1, last=True)
            rows_out(MG - 1)

        @block.scalar
        def _(act):
            def norm_power(w, n):
                act.wait_ge(norm_step[w], n * NORM + 3)
                nc.scalar.activation(log_var[:, w], var_eps[:, w], ACT.Ln).then_inc(norm_log[w], 1)
                act.wait_ge(norm_log[w], n + 1)
                nc.scalar.activation(rstd0[:, w], log_var[:, w], ACT.Exp, scale=-0.5).then_inc(norm_r0[w], 1)

            def step(t, par):
                odd = 1 - par
                n = t + 2
                if live(n):
                    norm_power(0, n)
                n = t - 3
                if live(n):
                    act.wait_ge(s_route, n * ROUTE + 2)
                    nc.scalar.activation(nexp[:], nabs[:], ACT.Exp, scale=-1.0).then_inc(s_noise_exp, 1)
                    act.wait_ge(s_noise_exp, n + 1)
                    nc.scalar.activation(nlog[:], nexp[:], ACT.Ln, bias=one[:]).then_inc(s_noise_log, 1)
                n = t + 1
                if live(n):
                    act.wait_ge(s_z1T_made, n + 1)
                    wait(act, s_v_made, n)
                    nc.scalar.activation(hT[:], ps[:, 4, :], ACT.Identity, bias=norm1[:, 1:2],
                                         scale=norm1[:, 0:1]).then_inc(s_hT_made, 1)
                n = t - 2
                if live(n):
                    act.wait_ge(s_z2T_made, n + 1)
                    wait(act, s_logits_made, n)
                    nc.scalar.activation(nT[:], ps[:, 6, :], ACT.Identity, bias=norm2[:, 1:2],
                                         scale=norm2[:, 0:1]).then_inc(s_nT_made, 1)
                n = t
                if live(n):
                    act.wait_ge(s_s_less, n + 1)
                    wait(act, s_p_norm, n)
                    nc.scalar.activation(probs[:], sc_m[:], ACT.Exp, scale=SCALE).then_inc(s_exp_made, 1)
                n = t - 3
                if live(n):
                    act.wait_ge(s_route, n * ROUTE + 11)
                    nc.scalar.activation(gexp[:], gdiff[:], ACT.Exp).then_inc(s_gate_exp, 1)
                n = t + 1
                if live(n):
                    act.wait_ge(s_q_made, n + 1)
                    wait(act, s_s_made, n)
                    nc.scalar.activation(qT[:], ps[:, 4, :], ACT.Copy).then_inc(s_q_copied, 1)
                    act.wait_ge(s_k_made, n + 1)
                    nc.scalar.activation(kT[:], ps[:, 6, :], ACT.Copy).then_inc(s_k_copied, 1)
                n = t - 1
                if live(n):
                    act.wait_ge(s_o_made, n + 1)
                    wait(act, s_wo_made, n)
                    nc.scalar.activation(oT[:], ps[:, 0:NB, P:2 * P].rearrange("c b (j t) -> c j b t", t=T),
                                         ACT.Copy).then_inc(s_oT_made, 1)
                n = t + 1
                if live(n):
                    act.wait_ge(s_v_made, n + 1)
                    wait(act, s_o_made, n - 1)
                    nc.scalar.activation(v_sb[:, odd].rearrange("p j c -> p (j c)"), ps[:, 5, :],
                                         ACT.Copy).then_inc(s_v_copied, 1)
                n = t - 1
                if live(n):
                    norm_power(1, n)

            act.wait_ge(s_consts_in, CONSTS)
            act.wait_ge(s_pool_consts, 1)
            pipeline(nc.scalar, step)

            def affine_rows(i):
                act.wait_ge(s_xgT_made, i + 1)
                wait(act, s_x_lo, i)
                nc.scalar.activation(x32[:], ps[:, 5, :], ACT.Identity, bias=norm2[:, 1:2],
                                     scale=norm2[:, 0:1]).then_inc(s_x32_made, 1)

            def experts(i, par, last=False):
                for c in range(CH):
                    act.wait_ge(s_h_made, i * CH + c + 1)
                    wait(act, s_h_lo, i * CH + c - 1)
                    nc.scalar.activation(h32[:, c % 2], ps[:, c, :], ACT.Relu,
                                         bias=bexp[:, par, c:c + 1]).then_inc(s_h32_made, 1)
                if not last:
                    affine_rows(i + 1)
                act.wait_ge(s_y_made, i + 1)
                wait(act, s_yrow_made, i)
                nc.scalar.activation(yT[:], ps[:, 4, :], ACT.Identity,
                                     bias=bexp[:, par, CH:CH + 1]).then_inc(s_yT_made, 1)

            affine_rows(0)
            experts(0, 0)
            with nc.scalar.Fori(1, MG - 2, 2) as i:
                experts(i, 1)
                experts(i + 1, 0)
            experts(MG - 1, 1, last=True)

            def store(n, par):
                act.wait_ge(s_f_made, n + 1)
                act.dma_start(out_t[:, bass.ds(n * J, J), :], fin[:, par]).then_inc(f_out[par], 16)

            with nc.scalar.Fori(0, NG - 1, 2) as n:
                store(n, 0)
                store(n + 1, 1)
            for q in f_out:
                act.wait_ge(q, 16 * NG // 2)

        @block.vector
        def _(dve):
            ev = nc.vector

            def norm_stats(w, n):
                for j in range(J):
                    m = ev.bn_stats(stats[:, w, j:j + 1], tile(xres, n, j))
                m.then_inc(norm_step[w], 1)
                apart(dve, (norm_step[w], n * NORM + 1))
                for j in range(J):
                    m = ev.bn_aggr(moments[:, w, j], stats[:, w, j])
                m.then_inc(norm_step[w], 1)
                dve.wait_ge(norm_step[w], n * NORM + 2)
                ev.tensor_scalar(var_eps[:, w], moments[:, w, :, 1], EPS, None, ALU.add).then_inc(norm_step[w], 1)

            def norm_rows(w, n, z):
                dve.wait_ge(norm_r0[w], n + 1)
                ev.tensor_tensor(newt_a[:, w], rstd0[:, w], rstd0[:, w], ALU.mult).then_inc(norm_step[w], 1)
                dve.wait_ge(norm_step[w], n * NORM + 4)
                ev.scalar_tensor_tensor(newt_b[:, w], newt_a[:, w], -0.5, var_eps[:, w], ALU.mult,
                                        ALU.mult).then_inc(norm_step[w], 1)
                dve.wait_ge(norm_step[w], n * NORM + 5)
                ev.scalar_tensor_tensor(rstd[:, w], newt_b[:, w], 1.5, rstd0[:, w], ALU.add,
                                        ALU.mult).then_inc(norm_step[w], 1)
                dve.wait_ge(norm_step[w], n * NORM + 6)
                for j in range(J):
                    m = ev.tensor_scalar(z[:, j:j + 1], tile(xres, n, j), moments[:, w, j, 0:1], rstd[:, w, j:j + 1],
                                         ALU.subtract, ALU.mult)
                m.then_inc(norm_step[w], 1)

            def step(t, par):
                odd = 1 - par
                n = t + 2
                if live(n):
                    apart(dve, (x_in[par], pair(n, par, 16) + 16))
                    norm_stats(0, n)
                n = t - 3
                if live(n):
                    dve.wait_ge(s_logits_made, n + 1)
                    ev.tensor_tensor(logit[:], ps[:, 7, 0:J * LW].rearrange("p (j l) -> p j l", j=J)[:, :, 0:NL],
                                     brouter[:].unsqueeze(1).to_broadcast([P, J, NL]), ALU.add).then_inc(s_route, 1)
                    dve.wait_ge(s_route, n * ROUTE + 1)
                    zn = logit[:, :, E:2 * E]
                    ev.scalar_tensor_tensor(nabs[:], zn, -1.0, zn, ALU.mult, ALU.max).then_inc(s_route, 1)
                n = t + 2
                if live(n):
                    wait(dve, s_z1T_made, n - 1)
                    norm_rows(0, n, z1[:, par])
                n = t - 3
                if live(n):
                    zn = logit[:, :, E:2 * E]
                    dve.wait_ge(s_noise_log, n + 1)
                    ev.scalar_tensor_tensor(spl[:], zn, 0.0, nlog[:], ALU.max, ALU.add).then_inc(s_route, 1)
                    dve.wait_ge(s_route, n * ROUTE + 3)
                    ev.tensor_tensor(nsp[:], spl[:], tiles(noise_sb, n), ALU.mult).then_inc(s_route, 1)
                    dve.wait_ge(s_route, n * ROUTE + 4)
                    ev.tensor_tensor(noisy[:], nsp[:], logit[:, :, 0:E], ALU.add).then_inc(s_route, 1)
                    apart(dve, (s_route, n * ROUTE + 5))
                    for j in range(J):
                        m = ev.max(top[:, j], noisy[:, j])
                    m.then_inc(s_route, 1)
                    apart(dve, (s_route, n * ROUTE + 6))
                    for j in range(J):
                        m = ev.max_index(top_i[:, j], top[:, j], noisy[:, j])
                    m.then_inc(s_route, 1)
                    dve.wait_ge(s_route, n * ROUTE + 7)
                    ev.tensor_copy(top_f[:], top_i[:, :, 0:K].rearrange("p j k -> p k j")).then_inc(s_route, 1)
                    dve.wait_ge(s_route, n * ROUTE + 8)
                    ev.tensor_tensor(hot[:].rearrange("p k j e -> p (k j) e"),
                                     top_f[:].rearrange("p k j -> p (k j)").unsqueeze(2).to_broadcast([P, K * J, E]),
                                     expert_no[:].unsqueeze(1).to_broadcast([P, K * J, E]),
                                     ALU.is_equal).then_inc(s_route, 1)
                    dve.wait_ge(s_route, n * ROUTE + 9)
                    wait(dve, s_rank_made, n)
                    ev.tensor_tensor(hot_any[:], hot[:, 0], hot[:, 1], ALU.add).then_inc(s_route, 1)
                    ev.tensor_tensor(gdiff[:], top[:, :, 1], top[:, :, 0], ALU.subtract).then_inc(s_route, 1)
                n = t
                if live(n):
                    dve.wait_ge(s_s_made, n + 1)
                    ev.tensor_tensor(sc[:], ps[:, 0:H, 0:P].rearrange("p h (j u) -> p h j u", u=T),
                                     causal[:].unsqueeze(1).unsqueeze(1).to_broadcast([P, H, J, T]),
                                     ALU.add).then_inc(s_s_masked, 1)
                    dve.wait_ge(s_s_masked, n + 1)
                    ev.tensor_reduce(smax[:], sc[:], AX.X, ALU.max).then_inc(s_s_max, 1)
                    dve.wait_ge(s_s_max, n + 1)
                    wait(dve, s_exp_made, n)
                    ev.tensor_tensor(sc_m[:], sc[:], smax[:].unsqueeze(3).to_broadcast([P, H, J, T]),
                                     ALU.subtract).then_inc(s_s_less, 1)
                n = t - 3
                if live(n):
                    ev.tensor_scalar(keep[:], logit[:, :, 2 * E], 0.0, None, ALU.is_le).then_inc(s_route, 1)
                    dve.wait_ge(s_gate_exp, n + 1)
                    ev.tensor_scalar(gden[:], gexp[:], 1.0, None, ALU.add).then_inc(s_route, 1)
                    dve.wait_ge(s_route, n * ROUTE + 13)
                    ev.reciprocal(gfirst[:], gden[:]).then_inc(s_route, 1)
                    dve.wait_ge(s_route, n * ROUTE + 14)
                    ev.tensor_tensor(tiles(gates, n)[:, :, 0:1], gfirst[:].unsqueeze(2), keep[:].unsqueeze(2),
                                     ALU.mult).then_inc(s_route, 1)
                    ev.tensor_tensor(gsecond[:], gexp[:], gfirst[:], ALU.mult).then_inc(s_route, 1)
                    dve.wait_ge(s_route, n * ROUTE + 16)
                    ev.tensor_tensor(tiles(gates, n)[:, :, 1:2], gsecond[:].unsqueeze(2), keep[:].unsqueeze(2),
                                     ALU.mult).then_inc(s_route, 1)
                n = t
                if live(n):
                    dve.wait_ge(s_exp_made, n + 1)
                    ev.tensor_reduce(psum_row[:], probs[:], AX.X, ALU.add).then_inc(s_p_sum, 1)
                    dve.wait_ge(s_p_sum, n + 1)
                    ev.reciprocal(prec[:], psum_row[:]).then_inc(s_p_inv, 1)
                    dve.wait_ge(s_p_inv, n + 1)
                    ev.tensor_tensor(pn[:], probs[:], prec[:].unsqueeze(3).to_broadcast([P, H, J, T]),
                                     ALU.mult).then_inc(s_p_norm, 1)
                    dve.wait_ge(s_p_norm, n + 1)
                    wait(dve, s_o_made, n - 1)
                    ev.transpose(pT[:, par].rearrange("p h j t -> p (h j t)"),
                                 pn[:].rearrange("p h j t -> p (h j t)")).then_inc(s_pT_made, 1)
                n = t - 3
                if live(n):
                    dve.wait_ge(s_rank_made, n + 1)
                    ev.tensor_tensor(rowno[:], ps[:, 7, 384:384 + J * E].rearrange("p (j e) -> p j e", e=E),
                                     fill[:].unsqueeze(1).to_broadcast([P, J, E]), ALU.add).then_inc(s_route, 1)
                    dve.wait_ge(s_route, n * ROUTE + 18)
                    for k in range(K):
                        m = ev.tensor_tensor(rowhot[:, k * J:(k + 1) * J], hot[:, k], rowno[:], ALU.mult)
                    m.then_inc(s_route, 1)
                    dve.wait_ge(s_route, n * ROUTE + 19)
                    wait(dve, sent[odd], pair(n, odd, SENT))
                    with nc.allow_low_precision(reason="a sum of row numbers below 2 ** 24"):
                        ev.tensor_reduce(rows_of[:, odd], rowhot[:], AX.X, ALU.add).then_inc(s_route, 1)
                    ev.tensor_tensor(fill[:], fill[:], ps[:, 7, 416:416 + E], ALU.add).then_inc(s_route, 1)
                n = t - 1
                if live(n):
                    dve.wait_ge(s_wo_made, n + 1)
                    dve.wait_ge(s_bo_added, n + 1)
                    ev.tensor_tensor(tiles(xres, n), ps[:, 4, :].rearrange("p (j c) -> p j c", j=J), tiles(xres, n),
                                     ALU.add).then_inc(s_x1_made, 1)
                    apart(dve, (s_x1_made, n + 1))
                    norm_stats(1, n)
                    wait(dve, s_z2T_made, n - 1)
                    wait(dve, s_pay_made, n - 1)
                    norm_rows(1, n, z2[:, odd])

            dve.wait_ge(s_pool_consts, 1)
            ev.tensor_reduce(causal[:], in_batch[:].rearrange("p b u -> p u b"), AX.X, ALU.add).then_inc(s_causal_made, 1)
            dve.wait_ge(s_causal_made, 1)
            dve.wait_ge(s_biases_in, 16 * 4)
            dve.wait_ge(s_noise_in, 16)
            pipeline(nc.vector, step)

            dve.wait_ge(s_route, NG * ROUTE)
            ev.tensor_tensor(count[:], fill[:], region_no[:], ALU.subtract).then_inc(s_table, 1)
            dve.wait_ge(s_table, 1)
            ev.tensor_tensor(over[:], count[:].unsqueeze(2).to_broadcast([P, E, NG]),
                             steps512[:].unsqueeze(1).to_broadcast([P, E, NG]), ALU.is_gt).then_inc(s_table, 1)
            dve.wait_ge(s_table, 2)
            ev.tensor_reduce(blocks_of[:], over[:], AX.X, ALU.add).then_inc(s_table, 1)
            dve.wait_ge(s_table, 3)
            ev.tensor_tensor(ends3[:], below[:], blocks_of[:].unsqueeze(1).to_broadcast([P, E, E]),
                             ALU.mult).then_inc(s_table, 1)
            dve.wait_ge(s_table, 4)
            ev.tensor_reduce(ends[:], ends3[:], AX.X, ALU.add).then_inc(s_table, 1)
            ev.tensor_scalar(jump[:], blocks_of[:], float(-G), float(ER), ALU.mult, ALU.add).then_inc(s_table, 1)
            dve.wait_ge(s_table, 6)
            ev.tensor_tensor(past[:], ends[:].unsqueeze(1).to_broadcast([P, MG, E]),
                             block_no[:].unsqueeze(2).to_broadcast([P, MG, E]), ALU.is_le).then_inc(s_table, 1)
            dve.wait_ge(s_table, 7)
            ev.tensor_tensor(past_jump[:], past[:], jump[:].unsqueeze(1).to_broadcast([P, MG, E]),
                             ALU.mult).then_inc(s_table, 1)
            ev.tensor_reduce(exp_f[:], past[:], AX.X, ALU.add).then_inc(s_table, 1)
            dve.wait_ge(s_table, 9)
            ev.tensor_reduce(row_part[:], past_jump[:], AX.X, ALU.add).then_inc(s_table, 1)
            ev.tensor_scalar(weights_at[:], exp_f[:], float(E - 1), float(P), ALU.min, ALU.mult).then_inc(s_table, 1)
            dve.wait_ge(s_table, 11)
            ev.scalar_tensor_tensor(rows_at[:], block_no[:], float(G), row_part[:], ALU.mult,
                                    ALU.add).then_inc(s_table, 1)
            ev.tensor_copy(fill_u[:], fill[:]).then_inc(s_table, 1)

            def split_rows(i, par):
                dve.wait_ge(s_x32_made, i + 1)
                wait(dve, s_h_made, (i - 1) * CH)
                ev.tensor_copy(xhi[:, par], x32[:]).then_inc(s_x_hi, 1)
                dve.wait_ge(s_x_hi, i + 1)
                ev.tensor_tensor(xlo[:, par], x32[:], xhi[:, par].bitcast(F32), ALU.subtract).then_inc(s_x_lo, 1)

            def copy_rows(i, par):
                dve.wait_ge(s_yrow_made, i + 1)
                wait(dve, res_out[par], pair(i, par, 16 * J))
                ev.tensor_copy(yrow[:, par].rearrange("p j c -> p (j c)"), ps[:, 6, :]).then_inc(s_yrow_copied, 1)

            def experts(i, par, first=False, last=False):
                wait(dve, s_y_made, i)
                for c in range(CH):
                    dve.wait_ge(s_h32_made, i * CH + c + 1)
                    ev.tensor_copy(hhi[:, c], h32[:, c % 2]).then_inc(s_h_hi, 1)
                    dve.wait_ge(s_h_hi, i * CH + c + 1)
                    ev.tensor_tensor(hlo[:, c], h32[:, c % 2], hhi[:, c].bitcast(F32), ALU.subtract).then_inc(s_h_lo, 1)
                    if c == 1:
                        wait(dve, res_out[par], pair(i, par, 16 * J))
                        ev.tensor_copy(words[:, par], xg_u[:, par, :, C]).then_inc(s_words_kept, 1)
                if not last:
                    split_rows(i + 1, 1 - par)
                if not first:
                    copy_rows(i - 1, 1 - par)

            split_rows(0, 0)
            experts(0, 0, first=True)
            experts(1, 1)
            experts(2, 0)
            with nc.vector.Fori(3, MG - 2, 2) as i:
                experts(i, 1)
                experts(i + 1, 0)
            experts(MG - 1, 1, last=True)
            copy_rows(MG - 1, 1)

            def combine(n, par):
                dve.wait_ge(f_in[par], pair(n, par, 32) + 32)
                for j in range(J):
                    m = ev.scalar_tensor_tensor(half[:, par, j:j + 1], yin[:, par, 0, j:j + 1],
                                                tile(gates, n, j)[:, 0, 0:1], tile(xres, n, j), ALU.mult, ALU.add)
                m.then_inc(s_f_half, 1)
                dve.wait_ge(s_f_half, n + 1)
                wait(dve, f_out[par], pair(n, par, 16))
                for j in range(J):
                    m = ev.scalar_tensor_tensor(fin[:, par, j:j + 1], yin[:, par, 1, j:j + 1],
                                                tile(gates, n, j)[:, 0, 1:2], half[:, par, j:j + 1], ALU.mult, ALU.add)
                m.then_inc(s_f_made, 1)

            combine(0, 0)
            combine(1, 1)
            with nc.vector.Fori(2, NG - 1, 2) as n:
                combine(n, 0)
                combine(n + 1, 1)

        @block.gpsimd
        def _(pool):
            g = nc.gpsimd
            g.memset(wrouter[:], 0.0).then_inc(s_router_zeroed, 1)
            g.memset(ident[:], 0.0).then_inc(s_ident_set, 1)
            g.memset(in_batch[:], 0.0).then_inc(s_mask_set, 1)
            g.memset(before[:], 1.0).then_inc(s_mask_set, 1)
            g.memset(below[:], 1.0).then_inc(s_mask_set, 1)
            g.memset(ones[:], 1.0)
            g.memset(one[:], 1.0)
            g.iota(expert_no[:], [[1, E]], base=0, channel_multiplier=0, allow_small_or_imprecise_dtypes=True)
            g.iota(fill[:], [[ER, E]], base=0, channel_multiplier=0, allow_small_or_imprecise_dtypes=True)
            g.iota(region_no[:], [[ER, E]], base=0, channel_multiplier=0, allow_small_or_imprecise_dtypes=True)
            g.iota(steps512[:], [[G, NG]], base=0, channel_multiplier=0, allow_small_or_imprecise_dtypes=True)
            g.iota(block_no[:], [[1, MG]], base=0, channel_multiplier=0, allow_small_or_imprecise_dtypes=True)
            pool.wait_ge(s_ident_set, 1)
            g.affine_select(ident[:], ident[:], pattern=[[-1, P]], compare_op=ALU.not_equal, fill=1.0, base=0,
                            channel_multiplier=1)
            pool.wait_ge(s_mask_set, 3)
            g.affine_select(in_batch[:], in_batch[:], pattern=[[-T, NB], [-1, T]], compare_op=ALU.is_ge, fill=NEG,
                            base=0, channel_multiplier=1).then_inc(s_batch_mask, 1)
            pool.wait_ge(s_batch_mask, 1)
            g.affine_select(in_batch[:], in_batch[:], pattern=[[-T, NB], [0, T]], compare_op=ALU.is_ge, fill=0.0,
                            base=0, channel_multiplier=1)
            g.affine_select(before[:], before[:], pattern=[[1, P]], compare_op=ALU.is_gt, fill=0.0, base=0,
                            channel_multiplier=-1)
            g.affine_select(below[:], below[:], pattern=[[1, E], [-1, E]], compare_op=ALU.is_ge, fill=0.0, base=0,
                            channel_multiplier=0).then_inc(s_pool_consts, 1)
            g.iota(token[:], [[N, K], [P, J]], base=0, channel_multiplier=1,
                   allow_small_or_imprecise_dtypes=True).then_inc(s_token_next, 1)
            g.memset(pay[:], 0.0).then_inc(s_pay_zeroed, 1)
            g.memset(blank[:], 0.0).then_inc(s_blank_set, 1)
            pool.wait_ge(s_blank_set, 1)
            g.iota(blank_u[:, :, C:C + 1], [[0, J]], base=FAR, channel_multiplier=0).then_inc(s_blank_word, 1)

            def load_raw(e):
                pool.dma_start(wraw[:, 0:HF], W1[e]).then_inc(s_raw_in, 16)
                pool.dma_start(wraw[:, HF:2 * HF].rearrange("p (k c) -> p k c", c=C),
                               W2[e].rearrange("(k p) c -> p k c", p=P)).then_inc(s_raw_in, 16)

            def split_weights(e):
                pool.wait_ge(s_raw_in, 32 * (e + 1))
                wait(pool, s_cut_out, 16 * e)
                g.tensor_copy(wcut[:, 0:2 * HF], wraw[:]).then_inc(s_cut_high, 1)
                pool.wait_ge(s_cut_high, e + 1)
                g.tensor_tensor(wcut[:, 2 * HF:4 * HF], wraw[:], wcut[:, 0:2 * HF].bitcast(F32),
                                ALU.subtract).then_inc(s_cut_low, 1)
                pool.wait_ge(s_cut_low, e + 1)
                pool.dma_start(wsplit[e * P:(e + 1) * P, :], wcut[:].bitcast(F32)).then_inc(s_cut_out, 16)
                if e + 1 < E:
                    load_raw(e + 1)

            def step(t, par):
                odd = 1 - par
                n = t - 2
                if live(n):
                    apart(pool, (s_norm2, (n + 1) * NORM),
                                (sent[par], pair(n, par, SENT)))
                    for k in range(K):
                        g.tensor_copy(pay[:, par, k, :, 0:C], z2[:, par])
                    apart(pool, (s_token_next, n + 1))
                    g.tensor_copy(pay_u[:, par, :, :, C], token[:]).then_inc(s_pay_made, 1)
                    apart(pool, (s_pay_made, n + 1))
                    g.tensor_scalar(token[:], token[:], float(G), None, ALU.add).then_inc(s_token_next, 1)
                n = t + 2
                if live(n):
                    apart(pool, (s_norm1, (n + 1) * NORM))
                    g.tensor_tensor(tiles(xres, n), tiles(xres, n), bo_row[:].unsqueeze(1).to_broadcast([P, J, C]),
                                    ALU.add).then_inc(s_bo_added, 1)
                n = t - 3
                if live(n):
                    apart(pool, (s_route, n * ROUTE + 20),
                                (s_pay_made, n + 1))
                    for k in range(K):
                        for j in range(J):
                            g.indirect_dma_start(rows, bass.IndirectOffsetOnAxis(
                                ap=rows_of[:, odd, k * J + j:k * J + j + 1], axis=0),
                                pay[:, odd, k, j, :], None).then_inc(sent[odd], 16)
                if isinstance(t, int):
                    e = t + 2 if t < NG // 2 else t - (NG - 3) + 7
                    if e < E:
                        split_weights(e)

            pool.wait_ge(s_pay_zeroed, 1)
            pool.wait_ge(s_biases_in, 16 * 4)
            load_raw(0)
            pipeline(nc.gpsimd, step)

            def scatter(i, par):
                apart(pool, (s_yrow_copied, i + 1))
                for j in range(J):
                    g.indirect_dma_start(results, bass.IndirectOffsetOnAxis(ap=words[:, par, j:j + 1], axis=0),
                                         yrow[:, par, j, :], None, bounds_check=K * N - 1,
                                         oob_is_err=False).then_inc(res_out[par], 16)

            with nc.gpsimd.Fori(0, MG - 1, 2) as i:
                scatter(i, 0)
                scatter(i + 1, 1)


_INS = ['r_x', 'r_noise', 'L0_rec_ln1_w', 'L0_rec_ln1_b', 'L0_rec_ln2_w', 'L0_rec_ln2_b', 'L0_rec_Wq', 'L0_rec_Wk',
        'L0_rec_Wv', 'L0_rec_Wo', 'L0_rec_bo', 'L0_rec_Wr', 'L0_rec_br', 'L0_rec_Wn', 'L0_rec_bn', 'L0_rec_Wsk',
        'L0_rec_bsk', 'L0_rec_W1', 'L0_rec_b1', 'L0_rec_W2', 'L0_rec_b2']


def kernel(**inputs):
    import numpy as _np
    import concourse.bacc as _bacc
    from concourse import mybir as _mybir
    from concourse.bass_utils import run_bass_kernel_spmd as _run

    nc = _bacc.Bacc("TRN2", target_bir_lowering=False, num_devices=1)
    arrays, args = {}, []
    for name in _INS:
        a = _np.ascontiguousarray(inputs[name])
        arrays[f"in_{name}"] = a
        args.append(nc.dram_tensor(f"in_{name}", a.shape, _mybir.dt.from_np(a.dtype), kind="ExternalInput").ap())
    out = nc.dram_tensor("out_0", inputs['r_x'].shape, _mybir.dt.float32, kind="ExternalOutput").ap()
    build(nc, *args, out)
    r = _run(nc, [arrays], core_ids=[0])
    return r.results[0]["out_0"]
```

```python
from contextlib import ExitStack

import concourse.bass as bass
from concourse import mybir

ALU = mybir.AluOpType
ACT = mybir.ActivationFunctionType
AX = mybir.AxisListType
F32 = mybir.dt.float32
F32R = mybir.dt.float32r
BF16 = mybir.dt.bfloat16
U32 = mybir.dt.uint32

P = 128
EPS = 1e-5
NEG = -1e30


def wait(eng, sem, value):
    if not (isinstance(value, int) and value <= 0):
        eng.wait_ge(sem, value)


def build(nc, x, noise, ln1_w, ln1_b, ln2_w, ln2_b, Wq, Wk, Wv, Wo, bo, Wr, br, Wn, bn, Wsk, bsk,
          W1, b1, W2, b2, out):
    B, T, C = x.shape
    H, _, HS = Wq.shape
    E, _, HF = W1.shape
    K = 2
    N = B * T
    J = 4
    G = J * P
    NG = N // G
    NB = P // T
    CH = HF // P
    MG = K * N // G + E
    ER = N + G
    RW = 132
    LW = 96
    NL = 2 * E + 1
    FAR = 1 << 24
    SCALE = float(C) ** -0.5
    assert C == P and HS == 32 and T == 32 and H * HS == C and NG % 4 == 0 and MG % 4 == 0

    xt = x.rearrange("b t c -> (b t) c").rearrange("(n p) c -> p n c", p=P)
    noise_t = noise.rearrange("b t e -> (b t) e").rearrange("(n p) e -> p n e", p=P)
    out_t = out.rearrange("b t c -> (b t) c").rearrange("(n p) c -> p n c", p=P)
    rows = nc.dram_tensor("expert_rows", [E * ER + E * G, RW], F32, kind="Internal").ap()
    results = nc.dram_tensor("expert_results", [K * N, C], F32, kind="Internal").ap()
    results_t = results.rearrange("(k n p) c -> p k n c", k=K, p=P)
    wsplit = nc.dram_tensor("split_weights", [E * P, 4 * HF], F32, kind="Internal").ap()
    biases = nc.dram_tensor("biases", [E * P, CH + 1], F32, kind="Internal").ap()

    ctx = ExitStack()
    with ctx:
        def sb(name, shape, dt=F32):
            return ctx.enter_context(nc.sbuf_tensor(name, shape, dt))

        def sem(name):
            return ctx.enter_context(nc.semaphore(name))

        ident = sb("ident", [P, P])
        before = sb("before", [P, P], BF16)
        ones = sb("ones", [P, P], BF16)
        zeros = sb("zeros", [P, P])
        causal = sb("causal", [P, T])
        in_batch = sb("in_batch", [P, NB, T])
        expert_no = sb("expert_no", [P, E])
        wq = sb("wq", [C, H, HS])
        wk = sb("wk", [C, H, HS])
        wv = sb("wv", [C, H, HS])
        wo = sb("wo", [C, C])
        wrouter = sb("wrouter", [C, LW])
        brouter = sb("brouter", [P, NL])
        bo_row = sb("bo_row", [P, C])
        norm1 = sb("norm1", [C, 2])
        norm2 = sb("norm2", [C, 2])
        one = sb("one", [P, 1])
        xres = sb("xres", [P, N // P, C])
        noise_sb = sb("noise_sb", [P, N // P, E])
        gates = sb("gates", [P, N // P, K])
        fill = sb("fill", [P, E])
        stats = sb("stats", [P, 2, J, 6])
        moments = sb("moments", [P, 2, J, 2])
        var_eps = sb("var_eps", [P, 2, J])
        log_var = sb("log_var", [P, 2, J])
        rstd0 = sb("rstd0", [P, 2, J])
        newt_a = sb("newt_a", [P, 2, J])
        newt_b = sb("newt_b", [P, 2, J])
        rstd = sb("rstd", [P, 2, J])
        z1 = sb("z1", [P, 2, J, C])
        z2 = sb("z2", [P, 2, J, C])
        hT = sb("hT", [C, G])
        qT = sb("qT", [C, G])
        kT = sb("kT", [C, G])
        v_sb = sb("v_sb", [P, 2, J, C])
        sc = sb("sc", [P, H, J, T])
        sc_m = sb("sc_m", [P, H, J, T])
        smax = sb("smax", [P, H, J])
        probs = sb("probs", [P, H, J, T])
        psum_row = sb("psum_row", [P, H, J])
        prec = sb("prec", [P, H, J])
        pn = sb("pn", [P, H, J, T])
        pT = sb("pT", [P, 2, H, J, T])
        oT = sb("oT", [C, J, NB, T])
        nT = sb("nT", [C, G])
        logit = sb("logit", [P, J, NL])
        nabs = sb("nabs", [P, J, E])
        nexp = sb("nexp", [P, J, E])
        nlog = sb("nlog", [P, J, E])
        spl = sb("spl", [P, J, E])
        nsp = sb("nsp", [P, J, E])
        noisy = sb("noisy", [P, J, E])
        top = sb("top", [P, J, 8])
        top_i = sb("top_i", [P, J, 8], U32)
        top_f = sb("top_f", [P, K, J])
        hot = sb("hot", [P, K, J, E])
        hot_any = sb("hot_any", [P, J, E], BF16)
        gdiff = sb("gdiff", [P, J])
        gexp = sb("gexp", [P, J])
        gden = sb("gden", [P, J])
        gfirst = sb("gfirst", [P, J])
        gsecond = sb("gsecond", [P, J])
        keep = sb("keep", [P, J])
        rowno = sb("rowno", [P, J, E])
        rowhot = sb("rowhot", [P, K * J, E])
        rows_of = sb("rows_of", [P, 2, K * J], U32)
        token = sb("token", [P, K, J])
        pay = sb("pay", [P, 2, K, J, RW])
        blocks_of = sb("blocks_of", [P, E])
        over = sb("over", [P, E, NG])
        steps512 = sb("steps512", [P, NG])
        below = sb("below", [P, E, E])
        ends3 = sb("ends3", [P, E, E])
        ends = sb("ends", [P, E])
        block_no = sb("block_no", [P, MG])
        past = sb("past", [P, MG, E])
        jump = sb("jump", [P, E])
        past_jump = sb("past_jump", [P, MG, E])
        exp_f = sb("exp_f", [P, MG])
        row_f = sb("row_f", [P, MG])
        weights_at = sb("weights_at", [P, MG], U32)
        rows_at = sb("rows_at", [P, MG], U32)
        fill_u = sb("fill_u", [P, E], U32)
        region_no = sb("region_no", [P, E])
        count = sb("count", [P, E])
        row_part = sb("row_part", [P, MG])
        blank = sb("blank", [P, J, RW])
        wraw = sb("wraw", [P, 2 * HF])
        wcut = sb("wcut", [P, 4 * HF], F32R)
        bias_t = sb("bias_t", [P, E, CH + 1])
        wexp = sb("wexp", [P, 2, 4 * HF], F32R)
        bexp = sb("bexp", [P, 2, CH + 1])
        x32 = sb("x32", [C, G])
        xhi = sb("xhi", [C, 2, G], F32R)
        xlo = sb("xlo", [C, 2, G], F32R)
        h32 = sb("h32", [P, 2, G])
        hhi = sb("hhi", [P, CH, G], F32R)
        hlo = sb("hlo", [P, CH, G], F32R)
        yT = sb("yT", [C, G])
        yin = [hhi[:, 0:K], hhi[:, K:2 * K], hlo[:, 0:K], hlo[:, K:2 * K]]
        yin = [y.rearrange("p k (j c) -> p k j c", c=C).bitcast(F32) for y in yin]
        half = z1
        fin = z2
        xg = [pay[:, i // 2, i % 2] for i in range(4)]
        yrow = [(z1, z2)[i // 2][:, i % 2] for i in range(4)]

        ps = ctx.enter_context(nc.psum_tensor("ps", [P, 8, 512], F32))

        s_x_in0 = sem("x_in0")
        s_x_in1 = sem("x_in1")
        s_consts_in = sem("consts_in")
        s_biases_in = sem("biases_in")
        s_ident_set = sem("ident_set")
        s_batch_mask = sem("batch_mask")
        s_causal_made = sem("causal_made")
        s_mask_set = sem("mask_set")
        s_pool_consts = sem("pool_consts")
        s_router_zeroed = sem("router_zeroed")
        s_noise_in = sem("noise_in")
        s_raw_in = sem("raw_in")
        s_cut_high = sem("cut_high")
        s_cut_low = sem("cut_low")
        s_cut_out = sem("cut_out")
        s_bias_out = sem("bias_out")
        s_blank_set = sem("blank_set")
        s_blank_word = sem("blank_word")
        s_blank_out = sem("blank_out")
        s_pay_zeroed = sem("pay_zeroed")
        s_norm1 = sem("norm1")
        s_norm1_log = sem("norm1_log")
        s_norm1_r0 = sem("norm1_r0")
        s_norm2 = sem("norm2")
        s_norm2_log = sem("norm2_log")
        s_norm2_r0 = sem("norm2_r0")
        s_z1T_made = sem("z1T_made")
        s_hT_made = sem("hT_made")
        s_q_made = sem("q_made")
        s_q_copied = sem("q_copied")
        s_k_made = sem("k_made")
        s_k_copied = sem("k_copied")
        s_v_made = sem("v_made")
        s_v_copied = sem("v_copied")
        s_s_made = sem("s_made")
        s_s_masked = sem("s_masked")
        s_s_max = sem("s_max")
        s_s_less = sem("s_less")
        s_exp_made = sem("exp_made")
        s_p_sum = sem("p_sum")
        s_p_inv = sem("p_inv")
        s_p_norm = sem("p_norm")
        s_pT_made = sem("pT_made")
        s_o_made = sem("o_made")
        s_oT_made = sem("oT_made")
        s_wo_made = sem("wo_made")
        s_x1_made = sem("x1_made")
        s_bo_added = sem("bo_added")
        s_z2T_made = sem("z2T_made")
        s_nT_made = sem("nT_made")
        s_logits_made = sem("logits_made")
        s_route = sem("route")
        s_noise_exp = sem("noise_exp")
        s_noise_log = sem("noise_log")
        s_gate_exp = sem("gate_exp")
        s_rank_made = sem("rank_made")
        s_pay_word = sem("pay_word")
        s_token_next = sem("token_next")
        s_pay_made = sem("pay_made")
        s_word_made = sem("word_made")
        s_sent0 = sem("sent0")
        s_sent1 = sem("sent1")
        s_table = sem("table")
        s_pads_out = sem("pads_out")
        s_e_in0 = sem("e_in0")
        s_e_in1 = sem("e_in1")
        s_e_in2 = sem("e_in2")
        s_e_in3 = sem("e_in3")
        s_w_in0 = sem("w_in0")
        s_w_in1 = sem("w_in1")
        s_xgT_made = sem("xgT_made")
        s_x32_made = sem("x32_made")
        s_x_hi = sem("x_hi")
        s_x_lo = sem("x_lo")
        s_h_made = sem("h_made")
        s_h32_made = sem("h32_made")
        s_h_hi = sem("h_hi")
        s_h_lo = sem("h_lo")
        s_y_made = sem("y_made")
        s_yT_made = sem("yT_made")
        s_yrow_made = sem("yrow_made")
        s_yrow_copied = sem("yrow_copied")
        s_res_out0 = sem("res_out0")
        s_res_out1 = sem("res_out1")
        s_res_out2 = sem("res_out2")
        s_res_out3 = sem("res_out3")
        s_f_in0 = sem("f_in0")
        s_f_in1 = sem("f_in1")
        s_f_in2 = sem("f_in2")
        s_f_in3 = sem("f_in3")
        s_f_half = sem("f_half")
        s_f_made = sem("f_made")
        s_f_out0 = sem("f_out0")
        s_f_out1 = sem("f_out1")
        norm_step, norm_log, norm_r0 = [s_norm1, s_norm2], [s_norm1_log, s_norm2_log], [s_norm1_r0, s_norm2_r0]
        x_in, sent, w_in = [s_x_in0, s_x_in1], [s_sent0, s_sent1], [s_w_in0, s_w_in1]
        e_in = [s_e_in0, s_e_in1, s_e_in2, s_e_in3]
        res_out = [s_res_out0, s_res_out1, s_res_out2, s_res_out3]
        f_in, f_out = [s_f_in0, s_f_in1, s_f_in2, s_f_in3], [s_f_out0, s_f_out1]
        NORM = 7
        ROUTE = 21
        SENT = 16 * K * J
        CONSTS = 16 * 11
        TABLE = 13

        pay_u = pay[:].bitcast(U32)
        blank_u = blank[:].bitcast(U32)

        def pair(n, par, per):
            if isinstance(n, int):
                return (n // 2) * per
            return n * (per // 2) - par * (per // 2)

        def quad(n, slot, per):
            if isinstance(n, int):
                return (n // 4) * per
            return n * (per // 4) - slot * (per // 4)

        def blocks(eng, body):
            for i in range(7):
                body(i, i % 4)
            with eng.Fori(7, MG - 4, 4) as i:
                for d in range(4):
                    body(i + d, (3 + d) % 4)
            body(MG - 1, 3)

        def tiles(a, n):
            return a[:, bass.ds(n * J, J), :]

        def tile(a, n, j):
            return a[:, bass.ds(n * J + j, 1), :]

        def pipeline(eng, step):
            for t in range(-2, 5):
                step(t, t % 2)
            with eng.Fori(5, NG - 4, 2) as t:
                step(t, 1)
                step(t + 1, 0)
            for t in range(NG - 3, NG + 3):
                step(t, t % 2)

        def apart(eng, *waits):
            known = [(q, v if isinstance(v, int) else eng.to_reg(v)) for q, v in waits]
            if not all(isinstance(v, int) for _, v in known):
                eng.wait_ge(s_pool_consts, 1)
            for q, v in known:
                wait(eng, q, v)

        def live(n):
            return not isinstance(n, int) or 0 <= n < NG

        def inner(i, other):
            return not isinstance(i, int) or 0 <= other < MG

        def upto(n):
            return min(n, NG) if isinstance(n, int) else n

        block = ctx.enter_context(nc.Block())

        @block.sync
        def _(sp):
            def load_x(n, par):
                apart(sp, (s_norm1, (n - 1) * NORM))
                sp.dma_start(tiles(xres, n), xt[:, bass.ds(n * J, J), :]).then_inc(x_in[par], 16)

            load_x(0, 0)
            load_x(1, 1)
            sp.dma_start(norm1[:, 0:1], ln1_w.unsqueeze(1)).then_inc(s_consts_in, 16)
            sp.dma_start(norm1[:, 1:2], ln1_b.unsqueeze(1)).then_inc(s_consts_in, 16)
            sp.dma_start(norm2[:, 0:1], ln2_w.unsqueeze(1)).then_inc(s_consts_in, 16)
            sp.dma_start(norm2[:, 1:2], ln2_b.unsqueeze(1)).then_inc(s_consts_in, 16)
            sp.dma_start(wq[:], Wq.rearrange("h c s -> c h s")).then_inc(s_consts_in, 16)
            sp.dma_start(wk[:], Wk.rearrange("h c s -> c h s")).then_inc(s_consts_in, 16)
            sp.dma_start(wv[:], Wv.rearrange("h c s -> c h s")).then_inc(s_consts_in, 16)
            sp.dma_start(wo[:], Wo).then_inc(s_consts_in, 16)
            sp.wait_ge(s_router_zeroed, 1)
            sp.dma_start(wrouter[:, 0:E], Wr).then_inc(s_consts_in, 16)
            sp.dma_start(wrouter[:, E:2 * E], Wn).then_inc(s_consts_in, 16)
            sp.dma_start(wrouter[:, 2 * E:NL], Wsk).then_inc(s_consts_in, 16)
            sp.dma_start(bo_row[:], bo.partition_broadcast(P)).then_inc(s_biases_in, 16)
            sp.dma_start(brouter[:, 0:E], br.partition_broadcast(P)).then_inc(s_biases_in, 16)
            sp.dma_start(brouter[:, E:2 * E], bn.partition_broadcast(P)).then_inc(s_biases_in, 16)
            sp.dma_start(brouter[:, 2 * E:NL], bsk.partition_broadcast(P)).then_inc(s_biases_in, 16)
            sp.dma_start(noise_sb[:], noise_t).then_inc(s_noise_in, 16)
            with sp.Fori(2, NG - 1, 2) as n:
                load_x(n, 0)
                load_x(n + 1, 1)

            with nc.allow_non_contiguous_dma(reason="a few KB of biases"):
                for e in range(E):
                    sp.dma_start(bias_t[:, e, 0:CH], b1[e].rearrange("(k p) -> p k", p=P)).then_inc(s_biases_in, 16)
                    sp.dma_start(bias_t[:, e, CH:CH + 1], b2[e].unsqueeze(1)).then_inc(s_biases_in, 16)
            sp.wait_ge(s_biases_in, 16 * (4 + 2 * E))
            sp.dma_start(biases.rearrange("(e p) k -> p e k", p=P), bias_t[:]).then_inc(s_bias_out, 16)

            sp.wait_ge(s_blank_word, 1)
            for e in range(E):
                sp.dma_start(rows[E * ER + e * G:E * ER + (e + 1) * G, :].rearrange("(p j) c -> p j c", j=J),
                             blank[:]).then_inc(s_blank_out, 16)
            sp.wait_ge(s_table, TABLE)
            for e in range(E):
                first = sp.value_load(fill_u[0:1, e:e + 1], min_val=0, max_val=E * ER - G)
                sp.dma_start(rows[bass.ds(first, G), :].rearrange("(p j) c -> p j c", j=J),
                             blank[:]).then_inc(s_pads_out, 16)

            sp.wait_ge(s_blank_out, 16 * E)
            sp.wait_ge(s_pads_out, 16 * E)
            sp.wait_ge(s_bias_out, 16)
            sp.wait_ge(s_cut_out, 16 * E)
            for q in sent:
                sp.wait_ge(q, SENT * NG // 2)

            def load_block(i, slot):
                row = sp.value_load(rows_at[0:1, bass.ds(i, 1)], min_val=0, max_val=E * ER + (E - 1) * G)
                at = sp.value_load(weights_at[0:1, bass.ds(i, 1)], min_val=0, max_val=(E - 1) * P)
                par = slot % 2
                apart(sp, (s_x32_made, i - 3),
                          (res_out[slot], quad(i, slot, 16 * J)))
                sp.dma_start(xg[slot], rows[bass.ds(row, G), :].rearrange("(p j) c -> p j c", j=J)
                             ).then_inc(e_in[slot], 16)
                apart(sp, (s_yT_made, i - 1))
                sp.dma_start(wexp[:, par].bitcast(F32), wsplit[bass.ds(at, P), :]).then_inc(w_in[par], 16)
                sp.dma_start(bexp[:, par], biases[bass.ds(at, P), :]).then_inc(w_in[par], 16)

            blocks(sp, load_block)

            for q in res_out:
                sp.wait_ge(q, 16 * J * MG // 4)

            def load_results(n, slot):
                apart(sp, (s_f_made, n - 3))
                for k in range(K):
                    sp.dma_start(yin[slot][:, k], results_t[:, k, bass.ds(n * J, J), :]).then_inc(f_in[slot], 16)

            for n in range(4):
                load_results(n, n)
            with sp.Fori(4, NG - 3, 4) as n:
                for d in range(4):
                    load_results(n + d, d)

        @block.tensor
        def _(pe):
            def transposes(to, of, ready):
                for j in range(J):
                    m = nc.tensor.transpose(to[:, j * P:(j + 1) * P], of[:, j], ident[:])
                m.then_inc(ready, 1)

            def step(t, par):
                odd = 1 - par
                n = t
                if live(n):
                    apart(pe, (s_k_copied, n + 1),
                              (s_oT_made, n - 1))
                    for j in range(J):
                        for b in range(NB):
                            for h in range(H):
                                at = slice(j * P + b * T, j * P + (b + 1) * T)
                                m = nc.tensor.matmul(ps[b * T:(b + 1) * T, h, j * T:(j + 1) * T],
                                                     qT[h * HS:(h + 1) * HS, at], kT[h * HS:(h + 1) * HS, at],
                                                     start=True, stop=True,
                                                     tile_position=(h * HS, b * T))
                    m.then_inc(s_s_made, 1)
                n = t + 1
                if live(n):
                    pe.wait_ge(s_norm1, (n + 1) * NORM)
                    wait(pe, s_x1_made, n - 2)
                    transposes(ps[:, 4, :], z1[:, odd], s_z1T_made)
                n = t - 2
                if live(n):
                    pe.wait_ge(s_norm2, (n + 1) * NORM)
                    wait(pe, s_k_copied, upto(n + 3))
                    transposes(ps[:, 6, :], z2[:, par], s_z2T_made)
                n = t + 1
                if live(n):
                    pe.wait_ge(s_hT_made, n + 1)
                    nc.tensor.matmul(ps[:, 4, :], wq[:].rearrange("c h s -> c (h s)"), hT[:],
                                     start=True, stop=True).then_inc(s_q_made, 1)
                    wait(pe, s_nT_made, n - 2)
                    nc.tensor.matmul(ps[:, 6, :], wk[:].rearrange("c h s -> c (h s)"), hT[:],
                                     start=True, stop=True).then_inc(s_k_made, 1)
                n = t - 3
                if live(n):
                    pe.wait_ge(s_route, n * ROUTE + 10)
                    wait(pe, s_route, n * ROUTE)
                    for j in range(J):
                        rank = ps[:, 7, 384 + j * E:384 + (j + 1) * E]
                        nc.tensor.matmul(rank, before[:], hot_any[:, j, :], start=True, stop=(j == 0))
                        for i in range(j):
                            nc.tensor.matmul(rank, ones[:], hot_any[:, i, :], start=False, stop=(i == j - 1))
                    for j in range(J):
                        m = nc.tensor.matmul(ps[:, 7, 416:416 + E], ones[:], hot_any[:, j, :],
                                             start=(j == 0), stop=(j == J - 1))
                    m.then_inc(s_rank_made, 1)
                n = t - 1
                if live(n):
                    apart(pe, (s_pT_made, n + 1),
                              (s_s_masked, upto(n + 2)))
                    for j in range(J):
                        for h in range(H):
                            for b in range(NB):
                                m = nc.tensor.matmul(ps[h * HS:(h + 1) * HS, b, P + j * T:P + (j + 1) * T],
                                                     v_sb[b * T:(b + 1) * T, odd, j, h * HS:(h + 1) * HS],
                                                     pT[b * T:(b + 1) * T, odd, h, j, :], start=True, stop=True,
                                                     tile_position=(b * T, h * HS))
                    m.then_inc(s_o_made, 1)
                n = t + 1
                if live(n):
                    wait(pe, s_v_copied, n)
                    for j in range(J):
                        m = nc.tensor.matmul(ps[:, 5, j * P:(j + 1) * P], hT[:, j * P:(j + 1) * P],
                                             wv[:].rearrange("c h s -> c (h s)"), start=True, stop=True)
                    m.then_inc(s_v_made, 1)
                n = t - 1
                if live(n):
                    pe.wait_ge(s_oT_made, n + 1)
                    wait(pe, s_q_copied, upto(n + 3))
                    for j in range(J):
                        m = nc.tensor.matmul(ps[:, 4, j * P:(j + 1) * P], oT[:, j].rearrange("c b t -> c (b t)"),
                                             wo[:], start=True, stop=True)
                    m.then_inc(s_wo_made, 1)
                n = t - 2
                if live(n):
                    pe.wait_ge(s_nT_made, n + 1)
                    wait(pe, s_route, n * ROUTE)
                    for j in range(J):
                        m = nc.tensor.matmul(ps[:, 7, j * LW:(j + 1) * LW], nT[:, j * P:(j + 1) * P], wrouter[:],
                                             start=True, stop=True)
                    m.then_inc(s_logits_made, 1)

            pe.wait_ge(s_pool_consts, 1)
            pe.wait_ge(s_consts_in, CONSTS)
            pipeline(nc.tensor, step)

            def rows_in(i, slot):
                pe.wait_ge(e_in[slot], quad(i, slot, 16) + 16)
                wait(pe, s_x32_made, i)
                transposes(ps[:, 5, :], xg[slot][:, :, 0:C], s_xgT_made)

            def rows_out(i):
                wait(pe, s_yT_made, i + 1)
                wait(pe, s_yrow_copied, i)
                transposes(ps[:, 6, :], yT[:].rearrange("c (j p) -> c j p", j=J), s_yrow_made)

            def experts(i, slot):
                par = slot % 2
                pe.wait_ge(s_x_lo, i + 1)
                pe.wait_ge(w_in[par], pair(i, par, 32) + 32)
                for c in range(CH):
                    w_hi = wexp[:, par, c * P:(c + 1) * P]
                    w_lo = wexp[:, par, 2 * HF + c * P:2 * HF + (c + 1) * P]
                    wait(pe, s_h32_made, (i - 1) * CH + c + 1)
                    nc.tensor.matmul(ps[:, c, :], w_hi, xhi[:, par], start=True, stop=False)
                    nc.tensor.matmul(ps[:, c, :], w_hi, xlo[:, par], start=False, stop=False)
                    nc.tensor.matmul(ps[:, c, :], w_lo, xhi[:, par], start=False, stop=True).then_inc(s_h_made, 1)
                if inner(i, i + 1):
                    rows_in(i + 1, (slot + 1) % 4)
                if inner(i, i - 1):
                    rows_out(i - 1)
                wait(pe, s_yT_made, i)
                for c in range(CH):
                    w_hi = wexp[:, par, HF + c * P:HF + (c + 1) * P]
                    w_lo = wexp[:, par, 3 * HF + c * P:3 * HF + (c + 1) * P]
                    pe.wait_ge(s_h_lo, i * CH + c + 1)
                    nc.tensor.matmul(ps[:, 4, :], w_hi, hhi[:, c], start=(c == 0), stop=False)
                    nc.tensor.matmul(ps[:, 4, :], w_lo, hhi[:, c], start=False, stop=False)
                    m = nc.tensor.matmul(ps[:, 4, :], w_hi, hlo[:, c], start=False, stop=(c == CH - 1))
                m.then_inc(s_y_made, 1)

            pe.wait_ge(s_route, NG * ROUTE)
            pe.wait_ge(s_x1_made, NG)
            pe.wait_ge(s_nT_made, NG)
            rows_in(0, 0)
            blocks(nc.tensor, experts)
            rows_out(MG - 1)

        @block.scalar
        def _(act):
            def norm_power(w, n):
                act.wait_ge(norm_step[w], n * NORM + 3)
                nc.scalar.activation(log_var[:, w], var_eps[:, w], ACT.Ln).then_inc(norm_log[w], 1)
                act.wait_ge(norm_log[w], n + 1)
                nc.scalar.activation(rstd0[:, w], log_var[:, w], ACT.Exp, scale=-0.5).then_inc(norm_r0[w], 1)

            def step(t, par):
                odd = 1 - par
                n = t + 2
                if live(n):
                    norm_power(0, n)
                n = t - 3
                if live(n):
                    act.wait_ge(s_route, n * ROUTE + 2)
                    nc.scalar.activation(nexp[:], nabs[:], ACT.Exp, scale=-1.0).then_inc(s_noise_exp, 1)
                    act.wait_ge(s_noise_exp, n + 1)
                    nc.scalar.activation(nlog[:], nexp[:], ACT.Ln, bias=one[:]).then_inc(s_noise_log, 1)
                n = t + 1
                if live(n):
                    act.wait_ge(s_z1T_made, n + 1)
                    wait(act, s_v_made, n)
                    nc.scalar.activation(hT[:], ps[:, 4, :], ACT.Identity, bias=norm1[:, 1:2],
                                         scale=norm1[:, 0:1]).then_inc(s_hT_made, 1)
                n = t - 2
                if live(n):
                    act.wait_ge(s_z2T_made, n + 1)
                    wait(act, s_logits_made, n)
                    nc.scalar.activation(nT[:], ps[:, 6, :], ACT.Identity, bias=norm2[:, 1:2],
                                         scale=norm2[:, 0:1]).then_inc(s_nT_made, 1)
                    wait(act, sent[par], pair(n, par, SENT))
                    nc.scalar.activation(pay[:, par, :, :, 0:C], z2[:, par].unsqueeze(1).to_broadcast([P, K, J, C]),
                                         ACT.Copy).then_inc(s_pay_made, 1)
                n = t
                if live(n):
                    act.wait_ge(s_s_less, n + 1)
                    wait(act, s_p_norm, n)
                    nc.scalar.activation(probs[:], sc_m[:], ACT.Exp, scale=SCALE).then_inc(s_exp_made, 1)
                n = t - 3
                if live(n):
                    act.wait_ge(s_route, n * ROUTE + 11)
                    nc.scalar.activation(gexp[:], gdiff[:], ACT.Exp).then_inc(s_gate_exp, 1)
                n = t + 1
                if live(n):
                    act.wait_ge(s_q_made, n + 1)
                    wait(act, s_s_made, n)
                    nc.scalar.activation(qT[:], ps[:, 4, :], ACT.Copy).then_inc(s_q_copied, 1)
                    act.wait_ge(s_k_made, n + 1)
                    nc.scalar.activation(kT[:], ps[:, 6, :], ACT.Copy).then_inc(s_k_copied, 1)
                n = t - 1
                if live(n):
                    act.wait_ge(s_o_made, n + 1)
                    wait(act, s_wo_made, n)
                    nc.scalar.activation(oT[:], ps[:, 0:NB, P:2 * P].rearrange("c b (j t) -> c j b t", t=T),
                                         ACT.Copy).then_inc(s_oT_made, 1)
                n = t + 1
                if live(n):
                    act.wait_ge(s_v_made, n + 1)
                    wait(act, s_o_made, n - 1)
                    nc.scalar.activation(v_sb[:, odd].rearrange("p j c -> p (j c)"), ps[:, 5, :],
                                         ACT.Copy).then_inc(s_v_copied, 1)
                n = t - 1
                if live(n):
                    norm_power(1, n)

            nc.scalar.preload_act_table_set("natural_log_exp_and_others")
            act.wait_ge(s_consts_in, CONSTS)
            act.wait_ge(s_pool_consts, 1)
            pipeline(nc.scalar, step)

            def affine_rows(i):
                act.wait_ge(s_xgT_made, i + 1)
                wait(act, s_x_lo, i)
                nc.scalar.activation(x32[:], ps[:, 5, :], ACT.Identity, bias=norm2[:, 1:2],
                                     scale=norm2[:, 0:1]).then_inc(s_x32_made, 1)

            def experts(i, slot):
                par = slot % 2
                for c in range(CH):
                    act.wait_ge(s_h_made, i * CH + c + 1)
                    wait(act, s_h_lo, i * CH + c - 1)
                    nc.scalar.activation(h32[:, c % 2], ps[:, c, :], ACT.Relu,
                                         bias=bexp[:, par, c:c + 1]).then_inc(s_h32_made, 1)
                if inner(i, i + 1):
                    affine_rows(i + 1)
                act.wait_ge(s_y_made, i + 1)
                wait(act, s_yrow_made, i)
                nc.scalar.activation(yT[:], ps[:, 4, :], ACT.Identity,
                                     bias=bexp[:, par, CH:CH + 1]).then_inc(s_yT_made, 1)

            affine_rows(0)
            blocks(nc.scalar, experts)

            def store(n, par):
                act.wait_ge(s_f_made, n + 1)
                act.dma_start(out_t[:, bass.ds(n * J, J), :], fin[:, par]).then_inc(f_out[par], 16)

            with nc.scalar.Fori(0, NG - 1, 2) as n:
                store(n, 0)
                store(n + 1, 1)
            for q in f_out:
                act.wait_ge(q, 16 * NG // 2)

        @block.vector
        def _(dve):
            ev = nc.vector

            def norm_stats(w, n):
                for j in range(J):
                    m = ev.bn_stats(stats[:, w, j:j + 1], tile(xres, n, j))
                m.then_inc(norm_step[w], 1)
                apart(dve, (norm_step[w], n * NORM + 1))
                for j in range(J):
                    m = ev.bn_aggr(moments[:, w, j], stats[:, w, j])
                m.then_inc(norm_step[w], 1)
                dve.wait_ge(norm_step[w], n * NORM + 2)
                ev.tensor_scalar(var_eps[:, w], moments[:, w, :, 1], EPS, None, ALU.add).then_inc(norm_step[w], 1)

            def norm_rows(w, n, z):
                dve.wait_ge(norm_r0[w], n + 1)
                ev.tensor_tensor(newt_a[:, w], rstd0[:, w], rstd0[:, w], ALU.mult).then_inc(norm_step[w], 1)
                dve.wait_ge(norm_step[w], n * NORM + 4)
                ev.scalar_tensor_tensor(newt_b[:, w], newt_a[:, w], -0.5, var_eps[:, w], ALU.mult,
                                        ALU.mult).then_inc(norm_step[w], 1)
                dve.wait_ge(norm_step[w], n * NORM + 5)
                ev.scalar_tensor_tensor(rstd[:, w], newt_b[:, w], 1.5, rstd0[:, w], ALU.add,
                                        ALU.mult).then_inc(norm_step[w], 1)
                dve.wait_ge(norm_step[w], n * NORM + 6)
                for j in range(J):
                    m = ev.tensor_scalar(z[:, j:j + 1], tile(xres, n, j), moments[:, w, j, 0:1], rstd[:, w, j:j + 1],
                                         ALU.subtract, ALU.mult)
                m.then_inc(norm_step[w], 1)

            def step(t, par):
                odd = 1 - par
                n = t + 2
                if live(n):
                    apart(dve, (x_in[par], pair(n, par, 16) + 16))
                    norm_stats(0, n)
                n = t - 3
                if live(n):
                    dve.wait_ge(s_logits_made, n + 1)
                    ev.tensor_tensor(logit[:], ps[:, 7, 0:J * LW].rearrange("p (j l) -> p j l", j=J)[:, :, 0:NL],
                                     brouter[:].unsqueeze(1).to_broadcast([P, J, NL]), ALU.add).then_inc(s_route, 1)
                    dve.wait_ge(s_route, n * ROUTE + 1)
                    zn = logit[:, :, E:2 * E]
                    ev.scalar_tensor_tensor(nabs[:], zn, -1.0, zn, ALU.mult, ALU.max).then_inc(s_route, 1)
                n = t + 2
                if live(n):
                    wait(dve, s_z1T_made, n - 1)
                    norm_rows(0, n, z1[:, par])
                n = t - 3
                if live(n):
                    zn = logit[:, :, E:2 * E]
                    dve.wait_ge(s_noise_log, n + 1)
                    ev.scalar_tensor_tensor(spl[:], zn, 0.0, nlog[:], ALU.max, ALU.add).then_inc(s_route, 1)
                    dve.wait_ge(s_route, n * ROUTE + 3)
                    ev.tensor_tensor(nsp[:], spl[:], tiles(noise_sb, n), ALU.mult).then_inc(s_route, 1)
                    dve.wait_ge(s_route, n * ROUTE + 4)
                    ev.tensor_tensor(noisy[:], nsp[:], logit[:, :, 0:E], ALU.add).then_inc(s_route, 1)
                    apart(dve, (s_route, n * ROUTE + 5))
                    for j in range(J):
                        m = ev.max(top[:, j], noisy[:, j])
                    m.then_inc(s_route, 1)
                    apart(dve, (s_route, n * ROUTE + 6))
                    for j in range(J):
                        m = ev.max_index(top_i[:, j], top[:, j], noisy[:, j])
                    m.then_inc(s_route, 1)
                    dve.wait_ge(s_route, n * ROUTE + 7)
                    ev.tensor_copy(top_f[:], top_i[:, :, 0:K].rearrange("p j k -> p k j")).then_inc(s_route, 1)
                    dve.wait_ge(s_route, n * ROUTE + 8)
                    ev.tensor_tensor(hot[:].rearrange("p k j e -> p (k j) e"),
                                     top_f[:].rearrange("p k j -> p (k j)").unsqueeze(2).to_broadcast([P, K * J, E]),
                                     expert_no[:].unsqueeze(1).to_broadcast([P, K * J, E]),
                                     ALU.is_equal).then_inc(s_route, 1)
                    dve.wait_ge(s_route, n * ROUTE + 9)
                    wait(dve, s_rank_made, n)
                    ev.tensor_tensor(hot_any[:], hot[:, 0], hot[:, 1], ALU.add).then_inc(s_route, 1)
                    ev.tensor_tensor(gdiff[:], top[:, :, 1], top[:, :, 0], ALU.subtract).then_inc(s_route, 1)
                n = t
                if live(n):
                    dve.wait_ge(s_s_made, n + 1)
                    ev.tensor_tensor(sc[:], ps[:, 0:H, 0:P].rearrange("p h (j u) -> p h j u", u=T),
                                     causal[:].unsqueeze(1).unsqueeze(1).to_broadcast([P, H, J, T]),
                                     ALU.add).then_inc(s_s_masked, 1)
                    dve.wait_ge(s_s_masked, n + 1)
                    ev.tensor_reduce(smax[:], sc[:], AX.X, ALU.max).then_inc(s_s_max, 1)
                    dve.wait_ge(s_s_max, n + 1)
                    wait(dve, s_exp_made, n)
                    ev.tensor_tensor(sc_m[:], sc[:], smax[:].unsqueeze(3).to_broadcast([P, H, J, T]),
                                     ALU.subtract).then_inc(s_s_less, 1)
                n = t - 3
                if live(n):
                    ev.tensor_scalar(keep[:], logit[:, :, 2 * E], 0.0, None, ALU.is_le).then_inc(s_route, 1)
                    dve.wait_ge(s_gate_exp, n + 1)
                    ev.tensor_scalar(gden[:], gexp[:], 1.0, None, ALU.add).then_inc(s_route, 1)
                    dve.wait_ge(s_route, n * ROUTE + 13)
                    ev.reciprocal(gfirst[:], gden[:]).then_inc(s_route, 1)
                    dve.wait_ge(s_route, n * ROUTE + 14)
                    ev.tensor_tensor(tiles(gates, n)[:, :, 0:1], gfirst[:].unsqueeze(2), keep[:].unsqueeze(2),
                                     ALU.mult).then_inc(s_route, 1)
                    ev.tensor_tensor(gsecond[:], gexp[:], gfirst[:], ALU.mult).then_inc(s_route, 1)
                    dve.wait_ge(s_route, n * ROUTE + 16)
                    ev.tensor_tensor(tiles(gates, n)[:, :, 1:2], gsecond[:].unsqueeze(2), keep[:].unsqueeze(2),
                                     ALU.mult).then_inc(s_route, 1)
                n = t
                if live(n):
                    dve.wait_ge(s_exp_made, n + 1)
                    ev.tensor_reduce(psum_row[:], probs[:], AX.X, ALU.add).then_inc(s_p_sum, 1)
                    dve.wait_ge(s_p_sum, n + 1)
                    ev.reciprocal(prec[:], psum_row[:]).then_inc(s_p_inv, 1)
                    dve.wait_ge(s_p_inv, n + 1)
                    ev.tensor_tensor(pn[:], probs[:], prec[:].unsqueeze(3).to_broadcast([P, H, J, T]),
                                     ALU.mult).then_inc(s_p_norm, 1)
                    dve.wait_ge(s_p_norm, n + 1)
                    wait(dve, s_o_made, n - 1)
                    ev.transpose(pT[:, par].rearrange("p h j t -> p (h j t)"),
                                 pn[:].rearrange("p h j t -> p (h j t)")).then_inc(s_pT_made, 1)
                n = t - 3
                if live(n):
                    dve.wait_ge(s_rank_made, n + 1)
                    ev.tensor_tensor(rowno[:], ps[:, 7, 384:384 + J * E].rearrange("p (j e) -> p j e", e=E),
                                     fill[:].unsqueeze(1).to_broadcast([P, J, E]), ALU.add).then_inc(s_route, 1)
                    dve.wait_ge(s_route, n * ROUTE + 18)
                    for k in range(K):
                        m = ev.tensor_tensor(rowhot[:, k * J:(k + 1) * J], hot[:, k], rowno[:], ALU.mult)
                    m.then_inc(s_route, 1)
                    dve.wait_ge(s_route, n * ROUTE + 19)
                    wait(dve, sent[odd], pair(n, odd, SENT))
                    with nc.allow_low_precision(reason="a sum of row numbers below 2 ** 24"):
                        ev.tensor_reduce(rows_of[:, odd], rowhot[:], AX.X, ALU.add).then_inc(s_route, 1)
                    ev.tensor_tensor(fill[:], fill[:], ps[:, 7, 416:416 + E], ALU.add).then_inc(s_route, 1)
                n = t - 1
                if live(n):
                    dve.wait_ge(s_wo_made, n + 1)
                    dve.wait_ge(s_bo_added, n + 1)
                    ev.tensor_tensor(tiles(xres, n), ps[:, 4, :].rearrange("p (j c) -> p j c", j=J), tiles(xres, n),
                                     ALU.add).then_inc(s_x1_made, 1)
                    apart(dve, (s_x1_made, n + 1))
                    norm_stats(1, n)
                    wait(dve, s_z2T_made, n - 1)
                    wait(dve, s_pay_made, n - 1)
                    norm_rows(1, n, z2[:, odd])

            dve.wait_ge(s_pool_consts, 1)
            ev.tensor_reduce(causal[:], in_batch[:].rearrange("p b u -> p u b"), AX.X, ALU.add).then_inc(s_causal_made, 1)
            dve.wait_ge(s_causal_made, 1)
            dve.wait_ge(s_biases_in, 16 * 4)
            dve.wait_ge(s_noise_in, 16)
            pipeline(nc.vector, step)

            dve.wait_ge(s_route, NG * ROUTE)
            ev.tensor_tensor(count[:], fill[:], region_no[:], ALU.subtract).then_inc(s_table, 1)
            dve.wait_ge(s_table, 1)
            ev.tensor_tensor(over[:], count[:].unsqueeze(2).to_broadcast([P, E, NG]),
                             steps512[:].unsqueeze(1).to_broadcast([P, E, NG]), ALU.is_gt).then_inc(s_table, 1)
            dve.wait_ge(s_table, 2)
            ev.tensor_reduce(blocks_of[:], over[:], AX.X, ALU.add).then_inc(s_table, 1)
            dve.wait_ge(s_table, 3)
            ev.tensor_tensor(ends3[:], below[:], blocks_of[:].unsqueeze(1).to_broadcast([P, E, E]),
                             ALU.mult).then_inc(s_table, 1)
            dve.wait_ge(s_table, 4)
            ev.tensor_reduce(ends[:], ends3[:], AX.X, ALU.add).then_inc(s_table, 1)
            ev.tensor_scalar(jump[:], blocks_of[:], float(-G), float(ER), ALU.mult, ALU.add).then_inc(s_table, 1)
            dve.wait_ge(s_table, 6)
            ev.tensor_tensor(past[:], ends[:].unsqueeze(1).to_broadcast([P, MG, E]),
                             block_no[:].unsqueeze(2).to_broadcast([P, MG, E]), ALU.is_le).then_inc(s_table, 1)
            dve.wait_ge(s_table, 7)
            ev.tensor_tensor(past_jump[:], past[:], jump[:].unsqueeze(1).to_broadcast([P, MG, E]),
                             ALU.mult).then_inc(s_table, 1)
            ev.tensor_reduce(exp_f[:], past[:], AX.X, ALU.add).then_inc(s_table, 1)
            dve.wait_ge(s_table, 9)
            ev.tensor_reduce(row_part[:], past_jump[:], AX.X, ALU.add).then_inc(s_table, 1)
            ev.tensor_scalar(weights_at[:], exp_f[:], float(E - 1), float(P), ALU.min, ALU.mult).then_inc(s_table, 1)
            dve.wait_ge(s_table, 11)
            ev.scalar_tensor_tensor(rows_at[:], block_no[:], float(G), row_part[:], ALU.mult,
                                    ALU.add).then_inc(s_table, 1)
            ev.tensor_copy(fill_u[:], fill[:]).then_inc(s_table, 1)

            def split_rows(i, par):
                dve.wait_ge(s_x32_made, i + 1)
                wait(dve, s_h_made, (i - 1) * CH)
                ev.tensor_copy(xhi[:, par], x32[:]).then_inc(s_x_hi, 1)
                dve.wait_ge(s_x_hi, i + 1)
                ev.tensor_tensor(xlo[:, par], x32[:], xhi[:, par].bitcast(F32), ALU.subtract).then_inc(s_x_lo, 1)

            def copy_rows(i, slot):
                dve.wait_ge(s_yrow_made, i + 1)
                wait(dve, res_out[slot], quad(i, slot, 16 * J))
                ev.tensor_copy(yrow[slot].rearrange("p j c -> p (j c)"), ps[:, 6, :]).then_inc(s_yrow_copied, 1)

            def experts(i, slot):
                wait(dve, s_y_made, i)
                for c in range(CH):
                    dve.wait_ge(s_h32_made, i * CH + c + 1)
                    ev.tensor_copy(hhi[:, c], h32[:, c % 2]).then_inc(s_h_hi, 1)
                    dve.wait_ge(s_h_hi, i * CH + c + 1)
                    ev.tensor_tensor(hlo[:, c], h32[:, c % 2], hhi[:, c].bitcast(F32), ALU.subtract).then_inc(s_h_lo, 1)
                if inner(i, i + 1):
                    split_rows(i + 1, (slot + 1) % 2)
                if inner(i, i - 1):
                    copy_rows(i - 1, (slot - 1) % 4)

            split_rows(0, 0)
            blocks(nc.vector, experts)
            copy_rows(MG - 1, 3)

            def combine(n, slot):
                par = slot % 2
                dve.wait_ge(f_in[slot], quad(n, slot, 16 * K) + 16 * K)
                for j in range(J):
                    m = ev.scalar_tensor_tensor(half[:, par, j:j + 1], yin[slot][:, 0, j:j + 1],
                                                tile(gates, n, j)[:, 0, 0:1], tile(xres, n, j), ALU.mult, ALU.add)
                m.then_inc(s_f_half, 1)
                dve.wait_ge(s_f_half, n + 1)
                wait(dve, f_out[par], pair(n, par, 16))
                for j in range(J):
                    m = ev.scalar_tensor_tensor(fin[:, par, j:j + 1], yin[slot][:, 1, j:j + 1],
                                                tile(gates, n, j)[:, 0, 1:2], half[:, par, j:j + 1], ALU.mult, ALU.add)
                m.then_inc(s_f_made, 1)

            for n in range(4):
                combine(n, n)
            with nc.vector.Fori(4, NG - 3, 4) as n:
                for d in range(4):
                    combine(n + d, d)

        @block.gpsimd
        def _(pool):
            g = nc.gpsimd
            g.memset(wrouter[:], 0.0).then_inc(s_router_zeroed, 1)
            g.memset(ident[:], 0.0).then_inc(s_ident_set, 1)
            g.memset(in_batch[:], 0.0).then_inc(s_mask_set, 1)
            g.memset(before[:], 1.0).then_inc(s_mask_set, 1)
            g.memset(below[:], 1.0).then_inc(s_mask_set, 1)
            g.memset(ones[:], 1.0)
            g.memset(one[:], 1.0)
            g.iota(expert_no[:], [[1, E]], base=0, channel_multiplier=0, allow_small_or_imprecise_dtypes=True)
            g.iota(fill[:], [[ER, E]], base=0, channel_multiplier=0, allow_small_or_imprecise_dtypes=True)
            g.iota(region_no[:], [[ER, E]], base=0, channel_multiplier=0, allow_small_or_imprecise_dtypes=True)
            g.iota(steps512[:], [[G, NG]], base=0, channel_multiplier=0, allow_small_or_imprecise_dtypes=True)
            g.iota(block_no[:], [[1, MG]], base=0, channel_multiplier=0, allow_small_or_imprecise_dtypes=True)
            pool.wait_ge(s_ident_set, 1)
            g.affine_select(ident[:], ident[:], pattern=[[-1, P]], compare_op=ALU.not_equal, fill=1.0, base=0,
                            channel_multiplier=1)
            pool.wait_ge(s_mask_set, 3)
            g.affine_select(in_batch[:], in_batch[:], pattern=[[-T, NB], [-1, T]], compare_op=ALU.is_ge, fill=NEG,
                            base=0, channel_multiplier=1).then_inc(s_batch_mask, 1)
            pool.wait_ge(s_batch_mask, 1)
            g.affine_select(in_batch[:], in_batch[:], pattern=[[-T, NB], [0, T]], compare_op=ALU.is_ge, fill=0.0,
                            base=0, channel_multiplier=1)
            g.affine_select(before[:], before[:], pattern=[[1, P]], compare_op=ALU.is_gt, fill=0.0, base=0,
                            channel_multiplier=-1)
            g.affine_select(below[:], below[:], pattern=[[1, E], [-1, E]], compare_op=ALU.is_ge, fill=0.0, base=0,
                            channel_multiplier=0).then_inc(s_pool_consts, 1)
            g.iota(token[:], [[N, K], [P, J]], base=0, channel_multiplier=1,
                   allow_small_or_imprecise_dtypes=True).then_inc(s_token_next, 1)
            g.memset(pay[:], 0.0).then_inc(s_pay_zeroed, 1)
            g.memset(blank[:], 0.0).then_inc(s_blank_set, 1)
            pool.wait_ge(s_blank_set, 1)
            g.iota(blank_u[:, :, C:C + 1], [[0, J]], base=FAR, channel_multiplier=0).then_inc(s_blank_word, 1)

            def load_raw(e):
                pool.dma_start(wraw[:, 0:HF], W1[e]).then_inc(s_raw_in, 16)
                pool.dma_start(wraw[:, HF:2 * HF].rearrange("p (k c) -> p k c", c=C),
                               W2[e].rearrange("(k p) c -> p k c", p=P)).then_inc(s_raw_in, 16)

            def split_weights(e):
                pool.wait_ge(s_raw_in, 32 * (e + 1))
                wait(pool, s_cut_out, 16 * e)
                g.tensor_copy(wcut[:, 0:2 * HF], wraw[:]).then_inc(s_cut_high, 1)
                pool.wait_ge(s_cut_high, e + 1)
                g.tensor_tensor(wcut[:, 2 * HF:4 * HF], wraw[:], wcut[:, 0:2 * HF].bitcast(F32),
                                ALU.subtract).then_inc(s_cut_low, 1)
                pool.wait_ge(s_cut_low, e + 1)
                pool.dma_start(wsplit[e * P:(e + 1) * P, :], wcut[:].bitcast(F32)).then_inc(s_cut_out, 16)
                if e + 1 < E:
                    load_raw(e + 1)

            def step(t, par):
                odd = 1 - par
                n = t - 2
                if live(n):
                    apart(pool, (sent[par], pair(n, par, SENT)),
                                (s_token_next, n + 1))
                    g.tensor_copy(pay_u[:, par, :, :, C], token[:]).then_inc(s_word_made, 1)
                    apart(pool, (s_word_made, n + 1))
                    g.tensor_scalar(token[:], token[:], float(G), None, ALU.add).then_inc(s_token_next, 1)
                n = t + 2
                if live(n):
                    apart(pool, (s_norm1, (n + 1) * NORM))
                    g.tensor_tensor(tiles(xres, n), tiles(xres, n), bo_row[:].unsqueeze(1).to_broadcast([P, J, C]),
                                    ALU.add).then_inc(s_bo_added, 1)
                n = t - 3
                if live(n):
                    apart(pool, (s_route, n * ROUTE + 20),
                                (s_pay_made, n + 1),
                                (s_word_made, n + 1))
                    for k in range(K):
                        for j in range(J):
                            g.indirect_dma_start(rows, bass.IndirectOffsetOnAxis(
                                ap=rows_of[:, odd, k * J + j:k * J + j + 1], axis=0),
                                pay[:, odd, k, j, :], None).then_inc(sent[odd], 16)
                if isinstance(t, int):
                    e = t + 2 if t < NG // 2 else t - (NG - 3) + 7
                    if e < E:
                        split_weights(e)

            pool.wait_ge(s_pay_zeroed, 1)
            pool.wait_ge(s_biases_in, 16 * 4)
            load_raw(0)
            pipeline(nc.gpsimd, step)

            def scatter(i, slot):
                apart(pool, (s_yrow_copied, i + 1))
                for j in range(J):
                    g.indirect_dma_start(results, bass.IndirectOffsetOnAxis(
                        ap=xg[slot][:, j, C:C + 1].bitcast(U32), axis=0),
                        yrow[slot][:, j, :], None, bounds_check=K * N - 1,
                        oob_is_err=False).then_inc(res_out[slot], 16)

            blocks(nc.gpsimd, scatter)


_INS = ['r_x', 'r_noise', 'L0_rec_ln1_w', 'L0_rec_ln1_b', 'L0_rec_ln2_w', 'L0_rec_ln2_b', 'L0_rec_Wq', 'L0_rec_Wk',
        'L0_rec_Wv', 'L0_rec_Wo', 'L0_rec_bo', 'L0_rec_Wr', 'L0_rec_br', 'L0_rec_Wn', 'L0_rec_bn', 'L0_rec_Wsk',
        'L0_rec_bsk', 'L0_rec_W1', 'L0_rec_b1', 'L0_rec_W2', 'L0_rec_b2']


def kernel(**inputs):
    import numpy as _np
    import concourse.bacc as _bacc
    from concourse import mybir as _mybir
    from concourse.bass_utils import run_bass_kernel_spmd as _run

    nc = _bacc.Bacc("TRN2", target_bir_lowering=False, num_devices=1)
    arrays, args = {}, []
    for name in _INS:
        a = _np.ascontiguousarray(inputs[name])
        arrays[f"in_{name}"] = a
        args.append(nc.dram_tensor(f"in_{name}", a.shape, _mybir.dt.from_np(a.dtype), kind="ExternalInput").ap())
    out = nc.dram_tensor("out_0", inputs['r_x'].shape, _mybir.dt.float32, kind="ExternalOutput").ap()
    build(nc, *args, out)
    r = _run(nc, [arrays], core_ids=[0])
    return r.results[0]["out_0"]
```

```python
from contextlib import ExitStack

import concourse.bass as bass
from concourse import mybir

ALU = mybir.AluOpType
ACT = mybir.ActivationFunctionType
AX = mybir.AxisListType
F32 = mybir.dt.float32
F32R = mybir.dt.float32r
BF16 = mybir.dt.bfloat16
U32 = mybir.dt.uint32

P = 128
EPS = 1e-5
NEG = -1e30


def wait(eng, sem, value):
    if not (isinstance(value, int) and value <= 0):
        eng.wait_ge(sem, value)


def build(nc, x, noise, ln1_w, ln1_b, ln2_w, ln2_b, Wq, Wk, Wv, Wo, bo, Wr, br, Wn, bn, Wsk, bsk,
          W1, b1, W2, b2, out):
    B, T, C = x.shape
    H, _, HS = Wq.shape
    E, _, HF = W1.shape
    K = 2
    N = B * T
    J = 4
    G = J * P
    NG = N // G
    NB = P // T
    CH = HF // P
    MG = K * N // G + E
    ER = N + G
    RW = 132
    LW = 96
    NL = 2 * E + 1
    FAR = 1 << 24
    BLANKS = 5
    SCALE = float(C) ** -0.5
    assert C == P and HS == 32 and T == 32 and H * HS == C and NG % 4 == 0 and MG % 4 == 0

    xt = x.rearrange("b t c -> (b t) c").rearrange("(n p) c -> p n c", p=P)
    noise_t = noise.rearrange("b t e -> (b t) e").rearrange("(n p) e -> p n e", p=P)
    out_t = out.rearrange("b t c -> (b t) c").rearrange("(n p) c -> p n c", p=P)
    rows = nc.dram_tensor("expert_rows", [E * ER + BLANKS * G, RW], F32, kind="Internal").ap()
    results = nc.dram_tensor("expert_results", [K * N, C], F32, kind="Internal").ap()
    results_t = results.rearrange("(k n p) c -> p k n c", k=K, p=P)
    wsplit1 = nc.dram_tensor("split_weights1", [E * P, 2 * HF + CH], F32, kind="Internal").ap()
    wsplit2 = nc.dram_tensor("split_weights2", [E * P, 2 * HF + 1], F32, kind="Internal").ap()

    ctx = ExitStack()
    with ctx:
        def sb(name, shape, dt=F32):
            return ctx.enter_context(nc.sbuf_tensor(name, shape, dt))

        def sem(name):
            return ctx.enter_context(nc.semaphore(name))

        ident = sb("ident", [P, P])
        before = sb("before", [P, P], BF16)
        ones = sb("ones", [P, P], BF16)
        zeros = sb("zeros", [P, P])
        filler = sb("filler", [P, 2 * P], BF16)
        causal = sb("causal", [P, T])
        in_batch = sb("in_batch", [P, NB, T])
        expert_no = sb("expert_no", [P, E])
        wq = sb("wq", [C, H, HS])
        wk = sb("wk", [C, H, HS])
        wv = sb("wv", [C, H, HS])
        wo = sb("wo", [C, C])
        wrouter = sb("wrouter", [C, LW])
        brouter = sb("brouter", [P, NL])
        bo_row = sb("bo_row", [P, C])
        norm1 = sb("norm1", [C, 2])
        norm2 = sb("norm2", [C, 2])
        one = sb("one", [P, 1])
        xres = sb("xres", [P, N // P, C])
        noise_sb = sb("noise_sb", [P, N // P, E])
        gates = sb("gates", [P, N // P, K])
        keep = sb("keep", [P, N // P])
        gdiff = sb("gdiff", [P, N // P])
        gexp = sb("gexp", [P, N // P])
        gden = sb("gden", [P, N // P])
        gfirst = sb("gfirst", [P, N // P])
        gsecond = sb("gsecond", [P, N // P])
        fill = sb("fill", [P, E])
        stats = sb("stats", [P, 2, J, 6])
        moments = sb("moments", [P, 2, J, 2])
        var_eps = sb("var_eps", [P, 2, J])
        log_var = sb("log_var", [P, 2, J])
        rstd0 = sb("rstd0", [P, 2, J])
        newt_a = sb("newt_a", [P, 2, J])
        newt_b = sb("newt_b", [P, 2, J])
        rstd = sb("rstd", [P, 2, J])
        shift = sb("shift", [P, 2, J])
        z1 = sb("z1", [P, 2, J, C])
        z2 = sb("z2", [P, 2, J, C])
        hT = sb("hT", [C, G])
        qT = sb("qT", [C, G])
        kT = sb("kT", [C, G])
        v_sb = sb("v_sb", [P, 2, J, C])
        sc = sb("sc", [P, H, J, T])
        sc_m = sb("sc_m", [P, H, J, T])
        smax = sb("smax", [P, H, J])
        probs = sb("probs", [P, H, J, T])
        psum_row = sb("psum_row", [P, H, J])
        prec = sb("prec", [P, H, J])
        pn = sb("pn", [P, H, J, T])
        pT = sb("pT", [P, 2, H, J, T])
        oT = sb("oT", [C, J, NB, T])
        nT = sb("nT", [C, G])
        logit = sb("logit", [P, J, NL])
        nabs = sb("nabs", [P, J, E])
        nexp = sb("nexp", [P, J, E])
        nlog = sb("nlog", [P, J, E])
        spl = sb("spl", [P, J, E])
        nsp = sb("nsp", [P, J, E])
        noisy = sb("noisy", [P, J, E])
        top = sb("top", [P, J, 8])
        top_i = sb("top_i", [P, J, 8], U32)
        top_f = sb("top_f", [P, K, J])
        far = sb("far", [P, J])
        row_sum = sb("row_sum", [P, K * J])
        hot = sb("hot", [P, K, J, E])
        hot_any = sb("hot_any", [P, J, E], BF16)
        rowno = sb("rowno", [P, J, E])
        rowhot = sb("rowhot", [P, K * J, E])
        rows_of = sb("rows_of", [P, 2, K * J], U32)
        token = sb("token", [P, K, J])
        pay = sb("pay", [P, 2, K, J, RW])
        blocks_of = sb("blocks_of", [P, E])
        over = sb("over", [P, E, NG])
        steps512 = sb("steps512", [P, NG])
        below = sb("below", [P, E, E])
        ends3 = sb("ends3", [P, E, E])
        ends = sb("ends", [P, E])
        block_no = sb("block_no", [P, MG + 1])
        fours = sb("fours", [P, MG // 4])
        fours_used = sb("fours_used", [P, MG // 4])
        fours_sum = sb("fours_sum", [P, 1])
        blocks_more = sb("blocks_more", [P, 1], U32)
        past = sb("past", [P, MG + 1, E])
        jump = sb("jump", [P, E])
        past_jump = sb("past_jump", [P, MG + 1, E])
        exp_f = sb("exp_f", [P, MG + 1])
        weights_at = sb("weights_at", [P, MG + 1], U32)
        rows_at = sb("rows_at", [P, MG + 1], U32)
        fill_u = sb("fill_u", [P, E], U32)
        region_no = sb("region_no", [P, E])
        count = sb("count", [P, E])
        row_part = sb("row_part", [P, MG + 1])
        blank = sb("blank", [P, J, RW])
        wraw = sb("wraw", [P, 2 * HF])
        bias_t = sb("bias_t", [P, E, CH + 1])
        w1x = sb("w1x", [P, 4, 2 * HF + CH], F32R)
        w2x = sb("w2x", [P, 4, 2 * HF + 1], F32R)
        wcut = w2x[:, 2:4, 0:2 * HF]
        words = sb("words", [P, 4, J], U32)
        x32 = sb("x32", [C, G])
        xhi = sb("xhi", [C, 2, G], F32R)
        xlo = sb("xlo", [C, 2, G], F32R)
        h32 = sb("h32", [P, 2, G])
        hhi = sb("hhi", [P, CH, G], F32R)
        hlo = sb("hlo", [P, CH, G], F32R)
        yT = sb("yT", [C, G])
        yin = [hhi[:, 0:K], hhi[:, K:2 * K], hlo[:, 0:K], hlo[:, K:2 * K]]
        yin = [y.rearrange("p k (j c) -> p k j c", c=C).bitcast(F32) for y in yin]
        half = z1
        fin = z2
        xg = [pay[:, i // 2, i % 2] for i in range(4)]
        yrow = [(z1, z2)[i // 2][:, i % 2] for i in range(4)]

        ps = ctx.enter_context(nc.psum_tensor("ps", [P, 8, 512], F32))

        s_x_in0 = sem("x_in0")
        s_x_in1 = sem("x_in1")
        s_consts_in = sem("consts_in")
        s_biases_in = sem("biases_in")
        s_ident_set = sem("ident_set")
        s_batch_mask = sem("batch_mask")
        s_causal_made = sem("causal_made")
        s_mask_set = sem("mask_set")
        s_pool_consts = sem("pool_consts")
        s_router_zeroed = sem("router_zeroed")
        s_noise_in = sem("noise_in")
        s_raw_in = sem("raw_in")
        s_cut_high = sem("cut_high")
        s_cut_low = sem("cut_low")
        s_cut_out = sem("cut_out")
        s_bias_out = sem("bias_out")
        s_blank_set = sem("blank_set")
        s_blank_word = sem("blank_word")
        s_blank_out = sem("blank_out")
        s_pay_zeroed = sem("pay_zeroed")
        s_norm = sem("norm")
        s_norm_log = sem("norm_log")
        s_norm_r0 = sem("norm_r0")
        s_z1 = sem("z1_made")
        s_z2 = sem("z2_made")
        s_z1T_made = sem("z1T_made")
        s_hT_made = sem("hT_made")
        s_q_made = sem("q_made")
        s_q_copied = sem("q_copied")
        s_k_made = sem("k_made")
        s_k_copied = sem("k_copied")
        s_v_made = sem("v_made")
        s_v_copied = sem("v_copied")
        s_s_made = sem("s_made")
        s_s_masked = sem("s_masked")
        s_s_max = sem("s_max")
        s_s_less = sem("s_less")
        s_exp_made = sem("exp_made")
        s_p_sum = sem("p_sum")
        s_p_inv = sem("p_inv")
        s_p_norm = sem("p_norm")
        s_pT_made = sem("pT_made")
        s_o_made = sem("o_made")
        s_oT_made = sem("oT_made")
        s_wo_made = sem("wo_made")
        s_x1_made = sem("x1_made")
        s_bo_added = sem("bo_added")
        s_z2T_made = sem("z2T_made")
        s_nT_made = sem("nT_made")
        s_logits_made = sem("logits_made")
        s_route = sem("route")
        s_noise_exp = sem("noise_exp")
        s_noise_log = sem("noise_log")
        s_rank_made = sem("rank_made")
        s_token_next = sem("token_next")
        s_pay_made = sem("pay_made")
        s_word_made = sem("word_made")
        s_sent0 = sem("sent0")
        s_sent1 = sem("sent1")
        s_table = sem("table")
        s_fill_u = sem("fill_u")
        s_gate_exp = sem("gate_exp")
        s_gate = sem("gate")
        s_pads_out = sem("pads_out")
        s_zeros_set = sem("zeros_set")
        s_results_zeroed = sem("results_zeroed")
        s_e_in0 = sem("e_in0")
        s_e_in1 = sem("e_in1")
        s_e_in2 = sem("e_in2")
        s_e_in3 = sem("e_in3")
        s_w1_in0 = sem("w1_in0")
        s_w1_in1 = sem("w1_in1")
        s_w1_in2 = sem("w1_in2")
        s_w1_in3 = sem("w1_in3")
        s_w2_in0 = sem("w2_in0")
        s_w2_in1 = sem("w2_in1")
        s_w2_in2 = sem("w2_in2")
        s_w2_in3 = sem("w2_in3")
        s_words_kept = sem("words_kept")
        s_xgT_made = sem("xgT_made")
        s_x32_made = sem("x32_made")
        s_x_hi = sem("x_hi")
        s_x_lo = sem("x_lo")
        s_h_made = sem("h_made")
        s_h32_made = sem("h32_made")
        s_h_hi = sem("h_hi")
        s_h_lo = sem("h_lo")
        s_y_part = sem("y_part")
        s_yT_made = sem("yT_made")
        s_yrow_made = sem("yrow_made")
        s_yrow_copied = sem("yrow_copied")
        s_res_out0 = sem("res_out0")
        s_res_out1 = sem("res_out1")
        s_res_out2 = sem("res_out2")
        s_res_out3 = sem("res_out3")
        s_f_in0 = sem("f_in0")
        s_f_in1 = sem("f_in1")
        s_f_in2 = sem("f_in2")
        s_f_in3 = sem("f_in3")
        s_f_half = sem("f_half")
        s_f_made = sem("f_made")
        s_f_out0 = sem("f_out0")
        s_f_out1 = sem("f_out1")
        x_in, sent = [s_x_in0, s_x_in1], [s_sent0, s_sent1]
        w1_in, w2_in = [s_w1_in0, s_w1_in1, s_w1_in2, s_w1_in3], [s_w2_in0, s_w2_in1, s_w2_in2, s_w2_in3]
        e_in = [s_e_in0, s_e_in1, s_e_in2, s_e_in3]
        res_out = [s_res_out0, s_res_out1, s_res_out2, s_res_out3]
        f_in, f_out = [s_f_in0, s_f_in1, s_f_in2, s_f_in3], [s_f_out0, s_f_out1]
        Y_BANKS = (4, 7)
        NORM = 7
        ROUTE = 18
        SENT = 16 * K * J
        CONSTS = 16 * 11
        TABLE = 16

        pay_u = pay[:].bitcast(U32)
        blank_u = blank[:].bitcast(U32)

        def pair(n, par, per):
            if isinstance(n, int):
                return (n // 2) * per
            return n * (per // 2) - par * (per // 2)

        def quad(n, slot, per):
            if isinstance(n, int):
                return (n // 4) * per
            return n * (per // 4) - slot * (per // 4)

        def blocks(eng, body):
            eng.wait_ge(s_table, TABLE)
            used = eng.value_load(blocks_more[0:1, 0:1], min_val=0, max_val=MG - 4) + 4
            for i in range(4):
                body(i, i)
            with eng.Fori(4, MG - 3, 4) as i:
                with eng.If(i < used):
                    for d in range(4):
                        body(i + d, d)
            return used

        def tiles(a, n):
            return a[:, bass.ds(n * J, J), :]

        def tile(a, n, j):
            return a[:, bass.ds(n * J + j, 1), :]

        def pipeline(eng, step):
            for t in range(-2, 5):
                step(t, t % 2)
            with eng.Fori(5, NG - 4, 2) as t:
                step(t, 1)
                step(t + 1, 0)
            for t in range(NG - 3, NG + 3):
                step(t, t % 2)

        def apart(eng, *waits):
            known = [(q, v if isinstance(v, int) else eng.to_reg(v)) for q, v in waits]
            if not all(isinstance(v, int) for _, v in known):
                eng.wait_ge(s_pool_consts, 1)
            for q, v in known:
                wait(eng, q, v)

        def live(n):
            return not isinstance(n, int) or 0 <= n < NG

        def splits(t):
            at = {**{e - 2: e for e in range(4)}, **{NG - 7 + e: e for e in range(4, E)}}
            return at.get(t) if isinstance(t, int) else None

        def has(i):
            return not isinstance(i, int) or i >= 0

        def upto(n):
            return min(n, NG) if isinstance(n, int) else n

        block = ctx.enter_context(nc.Block())

        @block.sync
        def _(sp):
            def load_x(n, par):
                apart(sp, (s_z1, n - 1))
                sp.dma_start(tiles(xres, n), xt[:, bass.ds(n * J, J), :]).then_inc(x_in[par], 16)

            def zero_results(n):
                sp.dma_start(results[bass.ds(n * K * G, K * G), :].rearrange("(p r) c -> p r c", p=P),
                             zeros[:].unsqueeze(1).to_broadcast([P, K * J, C])).then_inc(s_results_zeroed, 16)

            load_x(0, 0)
            load_x(1, 1)
            sp.dma_start(norm1[:, 0:1], ln1_w.unsqueeze(1)).then_inc(s_consts_in, 16)
            sp.dma_start(norm1[:, 1:2], ln1_b.unsqueeze(1)).then_inc(s_consts_in, 16)
            sp.dma_start(norm2[:, 0:1], ln2_w.unsqueeze(1)).then_inc(s_consts_in, 16)
            sp.dma_start(norm2[:, 1:2], ln2_b.unsqueeze(1)).then_inc(s_consts_in, 16)
            sp.dma_start(wq[:], Wq.rearrange("h c s -> c h s")).then_inc(s_consts_in, 16)
            sp.dma_start(wk[:], Wk.rearrange("h c s -> c h s")).then_inc(s_consts_in, 16)
            sp.dma_start(wv[:], Wv.rearrange("h c s -> c h s")).then_inc(s_consts_in, 16)
            sp.dma_start(wo[:], Wo).then_inc(s_consts_in, 16)
            sp.wait_ge(s_router_zeroed, 1)
            sp.dma_start(wrouter[:, 0:E], Wr).then_inc(s_consts_in, 16)
            sp.dma_start(wrouter[:, E:2 * E], Wn).then_inc(s_consts_in, 16)
            sp.dma_start(wrouter[:, 2 * E:NL], Wsk).then_inc(s_consts_in, 16)
            sp.dma_start(bo_row[:], bo.partition_broadcast(P)).then_inc(s_biases_in, 16)
            sp.dma_start(brouter[:, 0:E], br.partition_broadcast(P)).then_inc(s_biases_in, 16)
            sp.dma_start(brouter[:, E:2 * E], bn.partition_broadcast(P)).then_inc(s_biases_in, 16)
            sp.dma_start(brouter[:, 2 * E:NL], bsk.partition_broadcast(P)).then_inc(s_biases_in, 16)
            sp.dma_start(noise_sb[:], noise_t).then_inc(s_noise_in, 16)
            sp.wait_ge(s_zeros_set, 1)
            with sp.Fori(2, NG - 1, 2) as n:
                load_x(n, 0)
                zero_results(n)
                load_x(n + 1, 1)
                zero_results(n + 1)
            zero_results(0)
            zero_results(1)

            with nc.allow_non_contiguous_dma(reason="a few KB of biases"):
                for e in range(E):
                    sp.dma_start(bias_t[:, e, 0:CH], b1[e].rearrange("(k p) -> p k", p=P)).then_inc(s_biases_in, 16)
                    sp.dma_start(bias_t[:, e, CH:CH + 1], b2[e].unsqueeze(1)).then_inc(s_biases_in, 16)
            sp.wait_ge(s_biases_in, 16 * (4 + 2 * E))
            with nc.allow_non_contiguous_dma(reason="a few KB of biases"):
                sp.dma_start(wsplit1.rearrange("(e p) w -> p e w", p=P)[:, :, 2 * HF:],
                             bias_t[:, :, 0:CH]).then_inc(s_bias_out, 16)
                sp.dma_start(wsplit2.rearrange("(e p) w -> p e w", p=P)[:, :, 2 * HF:],
                             bias_t[:, :, CH:CH + 1]).then_inc(s_bias_out, 16)

            sp.wait_ge(s_blank_word, 1)
            for e in range(BLANKS):
                sp.dma_start(rows[E * ER + e * G:E * ER + (e + 1) * G, :].rearrange("(p j) c -> p j c", j=J),
                             blank[:]).then_inc(s_blank_out, 16)
            sp.wait_ge(s_fill_u, 1)
            for e in range(E):
                first = sp.value_load(fill_u[0:1, e:e + 1], min_val=0, max_val=E * ER - G)
                sp.dma_start(rows[bass.ds(first, G), :].rearrange("(p j) c -> p j c", j=J),
                             blank[:]).then_inc(s_pads_out, 16)

            sp.wait_ge(s_blank_out, 16 * BLANKS)
            sp.wait_ge(s_pads_out, 16 * E)
            sp.wait_ge(s_bias_out, 32)
            sp.wait_ge(s_table, TABLE)
            sp.wait_ge(s_cut_out, 32 * E)
            for q in sent:
                sp.wait_ge(q, SENT * NG // 2)

            def load_block(i, slot):
                row = sp.value_load(rows_at[0:1, bass.ds(i, 1)], min_val=0, max_val=E * ER + (BLANKS - 1) * G)
                at = sp.value_load(weights_at[0:1, bass.ds(i, 1)], min_val=0, max_val=(E - 1) * P)
                apart(sp, (s_x32_made, i - 3),
                          (s_words_kept, i - 3))
                sp.dma_start(xg[slot], rows[bass.ds(row, G), :].rearrange("(p j) c -> p j c", j=J)
                             ).then_inc(e_in[slot], 16)
                apart(sp, (s_yT_made, i - 3))
                sp.dma_start(w1x[:, slot].bitcast(F32), wsplit1[bass.ds(at, P), :]).then_inc(w1_in[slot], 16)
                sp.dma_start(w2x[:, slot].bitcast(F32), wsplit2[bass.ds(at, P), :]).then_inc(w2_in[slot], 16)

            load_block(0, 0)
            used = blocks(sp, lambda i, slot: load_block(i + 1, (slot + 1) % 4))

            apart(sp, *[(q, used * (16 * J // 4)) for q in res_out])

            def load_results(n, slot):
                apart(sp, (s_f_made, n - 3))
                for k in range(K):
                    sp.dma_start(yin[slot][:, k], results_t[:, k, bass.ds(n * J, J), :]).then_inc(f_in[slot], 16)

            for n in range(4):
                load_results(n, n)
            with sp.Fori(4, NG - 3, 4) as n:
                for d in range(4):
                    load_results(n + d, d)

        @block.tensor
        def _(pe):
            def transposes(to, of, ready):
                for j in range(J):
                    m = nc.tensor.transpose(to[:, j * P:(j + 1) * P], of[:, j], ident[:])
                m.then_inc(ready, 1)

            def keep_clock(times):
                for _ in range(times):
                    nc.tensor.matmul(ps[:, 0, 2 * P:4 * P], ones[:], filler[:], start=True, stop=True)

            def step(t, par):
                odd = 1 - par
                n = t
                if live(n):
                    apart(pe, (s_k_copied, n + 1),
                              (s_oT_made, n - 1),
                              (s_s_masked, n))
                    for j in range(J):
                        keep_clock(2)
                        for b in range(NB):
                            for h in range(H):
                                at = slice(j * P + b * T, j * P + (b + 1) * T)
                                m = nc.tensor.matmul(ps[b * T:(b + 1) * T, h, j * T:(j + 1) * T],
                                                     qT[h * HS:(h + 1) * HS, at], kT[h * HS:(h + 1) * HS, at],
                                                     start=True, stop=True,
                                                     tile_position=(h * HS, b * T))
                    m.then_inc(s_s_made, 1)
                n = t + 1
                if live(n):
                    pe.wait_ge(s_z1, n + 1)
                    wait(pe, s_x1_made, n - 2)
                    transposes(ps[:, 4, :], z1[:, odd], s_z1T_made)
                n = t + 1
                if live(n):
                    pe.wait_ge(s_hT_made, n + 1)
                    nc.tensor.matmul(ps[:, 4, :], wq[:].rearrange("c h s -> c (h s)"), hT[:],
                                     start=True, stop=True).then_inc(s_q_made, 1)
                    wait(pe, s_nT_made, n - 3)
                    nc.tensor.matmul(ps[:, 6, :], wk[:].rearrange("c h s -> c (h s)"), hT[:],
                                     start=True, stop=True).then_inc(s_k_made, 1)
                n = t - 1
                if live(n):
                    apart(pe, (s_pT_made, n + 1),
                              (s_s_masked, upto(n + 2)))
                    for j in range(J):
                        for h in range(H):
                            for b in range(NB):
                                m = nc.tensor.matmul(ps[h * HS:(h + 1) * HS, b, P + j * T:P + (j + 1) * T],
                                                     v_sb[b * T:(b + 1) * T, odd, j, h * HS:(h + 1) * HS],
                                                     pT[b * T:(b + 1) * T, odd, h, j, :], start=True, stop=True,
                                                     tile_position=(b * T, h * HS))
                    m.then_inc(s_o_made, 1)
                n = t - 3
                if live(n):
                    pe.wait_ge(s_route, n * ROUTE + 12)
                    wait(pe, s_route, n * ROUTE)
                    for j in range(J):
                        rank = ps[:, 7, 384 + j * E:384 + (j + 1) * E]
                        nc.tensor.matmul(rank, before[:], hot_any[:, j, :], start=True, stop=(j == 0))
                        for i in range(j):
                            nc.tensor.matmul(rank, ones[:], hot_any[:, i, :], start=False, stop=(i == j - 1))
                    for j in range(J):
                        m = nc.tensor.matmul(ps[:, 7, 416:416 + E], ones[:], hot_any[:, j, :],
                                             start=(j == 0), stop=(j == J - 1))
                    m.then_inc(s_rank_made, 1)
                n = t - 2
                if live(n):
                    pe.wait_ge(s_z2, n + 1)
                    wait(pe, s_k_copied, upto(n + 4))
                    transposes(ps[:, 6, :], z2[:, par], s_z2T_made)
                n = t + 1
                if live(n):
                    wait(pe, s_v_copied, n)
                    for j in range(J):
                        m = nc.tensor.matmul(ps[:, 5, j * P:(j + 1) * P], hT[:, j * P:(j + 1) * P],
                                             wv[:].rearrange("c h s -> c (h s)"), start=True, stop=True)
                    m.then_inc(s_v_made, 1)
                n = t - 1
                if live(n):
                    pe.wait_ge(s_oT_made, n + 1)
                    wait(pe, s_q_copied, upto(n + 3))
                    for j in range(J):
                        m = nc.tensor.matmul(ps[:, 4, j * P:(j + 1) * P], oT[:, j].rearrange("c b t -> c (b t)"),
                                             wo[:], start=True, stop=True)
                    m.then_inc(s_wo_made, 1)
                n = t - 2
                if live(n):
                    pe.wait_ge(s_nT_made, n + 1)
                    wait(pe, s_route, n * ROUTE)
                    for j in range(J):
                        m = nc.tensor.matmul(ps[:, 7, j * LW:(j + 1) * LW], nT[:, j * P:(j + 1) * P], wrouter[:],
                                             start=True, stop=True)
                    m.then_inc(s_logits_made, 1)

            pe.wait_ge(s_pool_consts, 1)
            pe.wait_ge(s_consts_in, CONSTS)
            pipeline(nc.tensor, step)

            def rows_in(i, slot):
                pe.wait_ge(e_in[slot], quad(i, slot, 16) + 16)
                wait(pe, s_x32_made, i)
                transposes(ps[:, 5, :], xg[slot][:, :, 0:C], s_xgT_made)

            def rows_out(i):
                wait(pe, s_yT_made, i + 1)
                wait(pe, s_yrow_copied, i)
                transposes(ps[:, 6, :], yT[:].rearrange("c (j p) -> c j p", j=J), s_yrow_made)

            def first_layer(i, slot, c):
                par = slot % 2
                w_hi = w1x[:, slot, c * P:(c + 1) * P]
                w_lo = w1x[:, slot, HF + c * P:HF + (c + 1) * P]
                if c == 0:
                    pe.wait_ge(s_x_lo, i + 1)
                    pe.wait_ge(w1_in[slot], quad(i, slot, 16) + 16)
                wait(pe, s_h_hi, (i - 1) * CH + c + 1)
                nc.tensor.matmul(ps[:, c, :], w_hi, xhi[:, par], start=True, stop=False)
                nc.tensor.matmul(ps[:, c, :], w_hi, xlo[:, par], start=False, stop=False)
                nc.tensor.matmul(ps[:, c, :], w_lo, xhi[:, par], start=False, stop=True).then_inc(s_h_made, 1)

            def second_layer(i, slot, c):
                w_hi = w2x[:, slot, c * P:(c + 1) * P]
                w_lo = w2x[:, slot, HF + c * P:HF + (c + 1) * P]
                if c == 0:
                    pe.wait_ge(w2_in[slot], quad(i, slot, 16) + 16)
                    wait(pe, s_yT_made, i - 1)
                pe.wait_ge(s_h_lo, i * CH + c + 1)
                bank = Y_BANKS[slot % 2]
                nc.tensor.matmul(ps[:, bank, :], w_hi, hhi[:, c], start=(c == 0), stop=False)
                nc.tensor.matmul(ps[:, bank, :], w_lo, hhi[:, c], start=False, stop=False)
                nc.tensor.matmul(ps[:, bank, :], w_hi, hlo[:, c], start=False, stop=(c == CH - 1)).then_inc(s_y_part, 1)

            def experts(i, slot):
                for c in range(CH):
                    if has(i - 1):
                        second_layer(i - 1, (slot - 1) % 4, c)
                    first_layer(i, slot, c)
                    if c == 0 and has(i - 2):
                        rows_out(i - 2)
                    if c == 1:
                        rows_in(i + 1, (slot + 1) % 4)

            pe.wait_ge(s_route, NG * ROUTE)
            pe.wait_ge(s_x1_made, NG)
            pe.wait_ge(s_nT_made, NG)
            rows_in(0, 0)
            used = blocks(nc.tensor, experts)
            for c in range(CH):
                second_layer(used - 1, 3, c)
                if c == 0:
                    rows_out(used - 2)
            rows_out(used - 1)

        @block.scalar
        def _(act):
            raw = wraw[:].rearrange("p (w f) -> p w f", w=2)

            def load_raw(e):
                act.dma_start(wraw[:, 0:HF], W1[e]).then_inc(s_raw_in, 16)
                act.dma_start(wraw[:, HF:2 * HF].rearrange("p (k c) -> p k c", c=C),
                              W2[e].rearrange("(k p) c -> p k c", p=P)).then_inc(s_raw_in, 16)

            def norm_rows(z, which, n):
                for j in range(J):
                    m = nc.scalar.activation(z[:, j:j + 1], tile(xres, n, j), ACT.Identity,
                                             bias=shift[:, which, j:j + 1], scale=rstd[:, which, j:j + 1])
                return m

            def step(t, par):
                odd = 1 - par
                if splits(t - 1) is not None:
                    e = splits(t - 1)
                    act.wait_ge(s_cut_low, e + 1)
                    for w, split in enumerate((wsplit1, wsplit2)):
                        act.dma_start(split[e * P:(e + 1) * P, 0:2 * HF], wcut[:, w].bitcast(F32)).then_inc(s_cut_out, 16)
                    if e + 1 < E:
                        load_raw(e + 1)
                which = slice(0 if live(t + 2) else 1, 2 if live(t - 2) else 1)
                if live(t + 2) or live(t - 2):
                    act.wait_ge(s_norm, (t + 2) * NORM + 3)
                    nc.scalar.activation(log_var[:, which], var_eps[:, which], ACT.Ln).then_inc(s_norm_log, 1)
                    act.wait_ge(s_norm_log, t + 3)
                    nc.scalar.activation(rstd0[:, which], log_var[:, which], ACT.Exp, scale=-0.5).then_inc(s_norm_r0, 1)
                n = t - 3
                if live(n):
                    act.wait_ge(s_route, n * ROUTE + 2)
                    nc.scalar.activation(nexp[:], nabs[:], ACT.Exp, scale=-1.0).then_inc(s_noise_exp, 1)
                    act.wait_ge(s_noise_exp, n + 1)
                    nc.scalar.activation(nlog[:], nexp[:], ACT.Ln, bias=one[:]).then_inc(s_noise_log, 1)
                n = t + 1
                if live(n):
                    act.wait_ge(s_z1T_made, n + 1)
                    wait(act, s_v_made, n)
                    nc.scalar.activation(hT[:], ps[:, 4, :], ACT.Identity, bias=norm1[:, 1:2],
                                         scale=norm1[:, 0:1]).then_inc(s_hT_made, 1)
                n = t - 2
                if live(n):
                    act.wait_ge(s_norm, (t + 3) * NORM)
                    wait(act, s_z2T_made, n - 1)
                    norm_rows(z2[:, par], 1, n).then_inc(s_z2, 1)
                n = t + 2
                if live(n):
                    act.wait_ge(s_norm, (t + 3) * NORM)
                    wait(act, s_z1T_made, n - 1)
                    norm_rows(z1[:, par], 0, n).then_inc(s_z1, 1)
                n = t + 1
                if live(n):
                    act.wait_ge(s_q_made, n + 1)
                    wait(act, s_s_made, n)
                    nc.scalar.activation(qT[:], ps[:, 4, :], ACT.Copy).then_inc(s_q_copied, 1)
                    act.wait_ge(s_k_made, n + 1)
                    nc.scalar.activation(kT[:], ps[:, 6, :], ACT.Copy).then_inc(s_k_copied, 1)
                n = t
                if live(n):
                    act.wait_ge(s_s_less, n + 1)
                    wait(act, s_p_norm, n)
                    nc.scalar.activation(probs[:], sc_m[:], ACT.Exp, scale=SCALE).then_inc(s_exp_made, 1)
                n = t - 1
                if live(n):
                    act.wait_ge(s_o_made, n + 1)
                    wait(act, s_wo_made, n)
                    nc.scalar.activation(oT[:], ps[:, 0:NB, P:2 * P].rearrange("c b (j t) -> c j b t", t=T),
                                         ACT.Copy).then_inc(s_oT_made, 1)
                n = t - 2
                if live(n):
                    act.wait_ge(s_z2T_made, n + 1)
                    wait(act, s_logits_made, n)
                    nc.scalar.activation(nT[:], ps[:, 6, :], ACT.Identity, bias=norm2[:, 1:2],
                                         scale=norm2[:, 0:1]).then_inc(s_nT_made, 1)
                n = t + 1
                if live(n):
                    act.wait_ge(s_v_made, n + 1)
                    wait(act, s_o_made, n - 1)
                    nc.scalar.activation(v_sb[:, odd].rearrange("p j c -> p (j c)"), ps[:, 5, :],
                                         ACT.Copy).then_inc(s_v_copied, 1)
                n = t - 2
                if live(n):
                    wait(act, sent[par], pair(n, par, SENT))
                    nc.scalar.activation(pay[:, par, :, :, 0:C], z2[:, par].unsqueeze(1).to_broadcast([P, K, J, C]),
                                         ACT.Copy).then_inc(s_pay_made, 1)

                e = splits(t)
                if e is not None:
                    act.wait_ge(s_raw_in, 32 * (e + 1))
                    wait(act, s_cut_out, 32 * e)
                    nc.scalar.activation(wcut[:, :, 0:HF], raw, ACT.Copy).then_inc(s_cut_high, 1)

            load_raw(0)
            nc.scalar.preload_act_table_set("natural_log_exp_and_others")
            act.wait_ge(s_consts_in, CONSTS)
            act.wait_ge(s_pool_consts, 1)
            pipeline(nc.scalar, step)

            act.wait_ge(s_route, NG * ROUTE)
            nc.scalar.activation(gexp[:], gdiff[:], ACT.Exp).then_inc(s_gate_exp, 1)

            def affine_rows(i):
                act.wait_ge(s_xgT_made, i + 1)
                wait(act, s_x_lo, i)
                nc.scalar.activation(x32[:], ps[:, 5, :], ACT.Identity, bias=norm2[:, 1:2],
                                     scale=norm2[:, 0:1]).then_inc(s_x32_made, 1)

            def experts(i, slot):
                for c in range(CH):
                    act.wait_ge(s_h_made, i * CH + c + 1)
                    wait(act, s_h_lo, i * CH + c - 1)
                    b1_c = w1x[:, slot, 2 * HF + c:2 * HF + c + 1].bitcast(F32)
                    nc.scalar.activation(h32[:, c % 2], ps[:, c, :], ACT.Relu, bias=b1_c).then_inc(s_h32_made, 1)
                    wait(act, s_y_part, (i - 1) * CH + c + 1)
                    nc.scalar.activation(hhi[:, c], ps[:, c, :], ACT.Relu, bias=b1_c).then_inc(s_h_hi, 1)
                    if c == 1:
                        affine_rows(i + 1)

            affine_rows(0)
            blocks(nc.scalar, experts)

            def store(n, par):
                act.wait_ge(s_f_made, n + 1)
                act.dma_start(out_t[:, bass.ds(n * J, J), :], fin[:, par]).then_inc(f_out[par], 16)

            with nc.scalar.Fori(0, NG - 1, 2) as n:
                store(n, 0)
                store(n + 1, 1)
            for q in f_out:
                act.wait_ge(q, 16 * NG // 2)

        @block.vector
        def _(dve):
            ev = nc.vector

            def step(t, par):
                odd = 1 - par
                norms = [(w, n) for w, n in ((1, t - 2), (0, t + 2)) if live(n)]
                which = slice(0 if live(t + 2) else 1, 2 if live(t - 2) else 1)
                base = (t + 2) * NORM
                n = t - 2
                if live(n):
                    dve.wait_ge(s_wo_made, n + 1)
                    dve.wait_ge(s_bo_added, n + 1)
                    ev.tensor_tensor(tiles(xres, n), ps[:, 4, :].rearrange("p (j c) -> p j c", j=J), tiles(xres, n),
                                     ALU.add).then_inc(s_x1_made, 1)
                if norms:
                    if live(t + 2):
                        apart(dve, (x_in[par], pair(t + 2, par, 16) + 16))
                        wait(dve, s_z1, t + 2)
                    for w, n in norms[::-1]:
                        if w == 1:
                            apart(dve, (s_x1_made, n + 1))
                            wait(dve, s_z2, n)
                        for j in range(J):
                            m = ev.bn_stats(stats[:, w, j:j + 1], tile(xres, n, j))
                    m.then_inc(s_norm, 1)
                    apart(dve, (s_norm, base + 1))
                    for w, n in norms:
                        for j in range(J):
                            m = ev.bn_aggr(moments[:, w, j], stats[:, w, j])
                    m.then_inc(s_norm, 1)
                n = t - 3
                if live(n):
                    dve.wait_ge(s_logits_made, n + 1)
                    ev.tensor_tensor(logit[:], ps[:, 7, 0:J * LW].rearrange("p (j l) -> p j l", j=J)[:, :, 0:NL],
                                     brouter[:].unsqueeze(1).to_broadcast([P, J, NL]), ALU.add).then_inc(s_route, 1)
                if norms:
                    dve.wait_ge(s_norm, base + 2)
                    ev.tensor_scalar(var_eps[:, which], moments[:, which, :, 1], EPS, None, ALU.add).then_inc(s_norm, 1)
                n = t - 3
                if live(n):
                    dve.wait_ge(s_route, n * ROUTE + 1)
                    zn = logit[:, :, E:2 * E]
                    ev.scalar_tensor_tensor(nabs[:], zn, -1.0, zn, ALU.mult, ALU.max).then_inc(s_route, 1)
                    ev.tensor_scalar(keep[:, bass.ds(n * J, J)], logit[:, :, 2 * E], 0.0, None,
                                     ALU.is_le).then_inc(s_route, 1)
                if norms:
                    dve.wait_ge(s_norm_r0, t + 3)
                    ev.tensor_tensor(newt_a[:, which], rstd0[:, which], rstd0[:, which], ALU.mult).then_inc(s_norm, 1)
                    dve.wait_ge(s_norm, base + 4)
                    ev.scalar_tensor_tensor(newt_b[:, which], newt_a[:, which], -0.5, var_eps[:, which], ALU.mult,
                                            ALU.mult).then_inc(s_norm, 1)
                    dve.wait_ge(s_norm, base + 5)
                    ev.scalar_tensor_tensor(rstd[:, which], newt_b[:, which], 1.5, rstd0[:, which], ALU.add,
                                            ALU.mult).then_inc(s_norm, 1)
                    dve.wait_ge(s_norm, base + 6)
                    ev.scalar_tensor_tensor(shift[:, which], moments[:, which, :, 0], -1.0, rstd[:, which], ALU.mult,
                                            ALU.mult).then_inc(s_norm, 1)
                n = t
                if live(n):
                    dve.wait_ge(s_s_made, n + 1)
                    ev.tensor_tensor(sc[:], ps[:, 0:H, 0:P].rearrange("p h (j u) -> p h j u", u=T),
                                     causal[:].unsqueeze(1).unsqueeze(1).to_broadcast([P, H, J, T]),
                                     ALU.add).then_inc(s_s_masked, 1)
                    dve.wait_ge(s_s_masked, n + 1)
                    ev.tensor_reduce(smax[:], sc[:], AX.X, ALU.max).then_inc(s_s_max, 1)
                    dve.wait_ge(s_s_max, n + 1)
                    wait(dve, s_exp_made, n)
                    ev.tensor_tensor(sc_m[:], sc[:], smax[:].unsqueeze(3).to_broadcast([P, H, J, T]),
                                     ALU.subtract).then_inc(s_s_less, 1)
                n = t - 3
                if live(n):
                    zn = logit[:, :, E:2 * E]
                    dve.wait_ge(s_noise_log, n + 1)
                    if isinstance(n, int) and n == 0:
                        dve.wait_ge(s_noise_in, 16)
                    ev.scalar_tensor_tensor(spl[:], zn, 0.0, nlog[:], ALU.max, ALU.add).then_inc(s_route, 1)
                    dve.wait_ge(s_route, n * ROUTE + 4)
                    ev.tensor_tensor(nsp[:], spl[:], tiles(noise_sb, n), ALU.mult).then_inc(s_route, 1)
                    dve.wait_ge(s_route, n * ROUTE + 5)
                    ev.tensor_tensor(noisy[:], nsp[:], logit[:, :, 0:E], ALU.add).then_inc(s_route, 1)
                    apart(dve, (s_route, n * ROUTE + 6))
                    for j in range(J):
                        m = ev.max(top[:, j], noisy[:, j])
                    m.then_inc(s_route, 1)
                    apart(dve, (s_route, n * ROUTE + 7))
                    for j in range(J):
                        m = ev.max_index(top_i[:, j], top[:, j], noisy[:, j])
                    m.then_inc(s_route, 1)
                    ev.tensor_tensor(gdiff[:, bass.ds(n * J, J)], top[:, :, 1], top[:, :, 0],
                                     ALU.subtract).then_inc(s_route, 1)
                    dve.wait_ge(s_route, n * ROUTE + 8)
                    ev.scalar_tensor_tensor(top_f[:], top_i[:, :, 0:K].rearrange("p j k -> p k j"), 1.0,
                                            keep[:, bass.ds(n * J, J)].unsqueeze(1).to_broadcast([P, K, J]),
                                            ALU.add, ALU.mult).then_inc(s_route, 1)
                    dve.wait_ge(s_route, n * ROUTE + 10)
                    ev.tensor_tensor(hot[:].rearrange("p k j e -> p (k j) e"),
                                     top_f[:].rearrange("p k j -> p (k j)").unsqueeze(2).to_broadcast([P, K * J, E]),
                                     expert_no[:].unsqueeze(1).to_broadcast([P, K * J, E]),
                                     ALU.is_equal).then_inc(s_route, 1)
                    dve.wait_ge(s_route, n * ROUTE + 11)
                    wait(dve, s_rank_made, n)
                    ev.tensor_tensor(hot_any[:], hot[:, 0], hot[:, 1], ALU.add).then_inc(s_route, 1)
                    ev.tensor_scalar(far[:], keep[:, bass.ds(n * J, J)], -float(FAR), float(FAR), ALU.mult,
                                     ALU.add).then_inc(s_route, 1)
                n = t
                if live(n):
                    dve.wait_ge(s_exp_made, n + 1)
                    ev.tensor_reduce(psum_row[:], probs[:], AX.X, ALU.add).then_inc(s_p_sum, 1)
                    dve.wait_ge(s_p_sum, n + 1)
                    wait(dve, s_p_norm, n)
                    ev.reciprocal(prec[:], psum_row[:]).then_inc(s_p_inv, 1)
                n = t - 3
                if live(n):
                    dve.wait_ge(s_rank_made, n + 1)
                    ev.tensor_tensor(rowno[:], ps[:, 7, 384:384 + J * E].rearrange("p (j e) -> p j e", e=E),
                                     fill[:].unsqueeze(1).to_broadcast([P, J, E]), ALU.add).then_inc(s_route, 1)
                    dve.wait_ge(s_route, n * ROUTE + 14)
                    for k in range(K):
                        m = ev.tensor_tensor(rowhot[:, k * J:(k + 1) * J], hot[:, k], rowno[:], ALU.mult)
                    m.then_inc(s_route, 1)
                    ev.tensor_tensor(fill[:], fill[:], ps[:, 7, 416:416 + E], ALU.add).then_inc(s_route, 1)
                    dve.wait_ge(s_route, n * ROUTE + 15)
                    ev.tensor_reduce(row_sum[:], rowhot[:], AX.X, ALU.add).then_inc(s_route, 1)
                    dve.wait_ge(s_route, n * ROUTE + 17)
                    wait(dve, sent[odd], pair(n, odd, SENT))
                    ev.tensor_tensor(rows_of[:, odd].rearrange("p (k j) -> p k j", k=K),
                                     row_sum[:].rearrange("p (k j) -> p k j", k=K),
                                     far[:].unsqueeze(1).to_broadcast([P, K, J]), ALU.add).then_inc(s_route, 1)
                n = t
                if live(n):
                    dve.wait_ge(s_p_norm, n + 1)
                    wait(dve, s_o_made, n - 1)
                    ev.transpose(pT[:, par].rearrange("p h j t -> p (h j t)"),
                                 pn[:].rearrange("p h j t -> p (h j t)")).then_inc(s_pT_made, 1)

                e = splits(t)
                if e is not None:
                    dve.wait_ge(s_cut_high, e + 1)
                    ev.tensor_tensor(wcut[:, :, HF:2 * HF], wraw[:].rearrange("p (w f) -> p w f", w=2),
                                     wcut[:, :, 0:HF].bitcast(F32), ALU.subtract).then_inc(s_cut_low, 1)

            dve.wait_ge(s_pool_consts, 1)
            ev.tensor_reduce(causal[:], in_batch[:].rearrange("p b u -> p u b"), AX.X, ALU.add).then_inc(s_causal_made, 1)
            dve.wait_ge(s_causal_made, 1)
            dve.wait_ge(s_biases_in, 16 * 4)
            pipeline(nc.vector, step)

            dve.wait_ge(s_route, NG * ROUTE)
            ev.tensor_copy(fill_u[:], fill[:]).then_inc(s_fill_u, 1)
            ev.tensor_tensor(count[:], fill[:], region_no[:], ALU.subtract).then_inc(s_table, 1)
            dve.wait_ge(s_table, 1)
            ev.tensor_tensor(over[:], count[:].unsqueeze(2).to_broadcast([P, E, NG]),
                             steps512[:].unsqueeze(1).to_broadcast([P, E, NG]), ALU.is_gt).then_inc(s_table, 1)
            dve.wait_ge(s_table, 2)
            ev.tensor_reduce(blocks_of[:], over[:], AX.X, ALU.add).then_inc(s_table, 1)
            dve.wait_ge(s_table, 3)
            ev.tensor_tensor(ends3[:], below[:], blocks_of[:].unsqueeze(1).to_broadcast([P, E, E]),
                             ALU.mult).then_inc(s_table, 1)
            dve.wait_ge(s_table, 4)
            ev.tensor_reduce(ends[:], ends3[:], AX.X, ALU.add).then_inc(s_table, 1)
            ev.tensor_scalar(jump[:], blocks_of[:], float(-G), float(ER), ALU.mult, ALU.add).then_inc(s_table, 1)
            dve.wait_ge(s_table, 6)
            ev.tensor_tensor(past[:], ends[:].unsqueeze(1).to_broadcast([P, MG + 1, E]),
                             block_no[:].unsqueeze(2).to_broadcast([P, MG + 1, E]), ALU.is_le).then_inc(s_table, 1)
            dve.wait_ge(s_table, 7)
            ev.tensor_tensor(past_jump[:], past[:], jump[:].unsqueeze(1).to_broadcast([P, MG + 1, E]),
                             ALU.mult).then_inc(s_table, 1)
            ev.tensor_reduce(exp_f[:], past[:], AX.X, ALU.add).then_inc(s_table, 1)
            dve.wait_ge(s_table, 9)
            ev.tensor_reduce(row_part[:], past_jump[:], AX.X, ALU.add).then_inc(s_table, 1)
            ev.tensor_scalar(weights_at[:], exp_f[:], float(E - 1), float(P), ALU.min, ALU.mult).then_inc(s_table, 1)
            dve.wait_ge(s_table, 11)
            ev.scalar_tensor_tensor(rows_at[:], block_no[:], float(G), row_part[:], ALU.mult,
                                    ALU.add).then_inc(s_table, 1)
            ev.tensor_tensor(fours_used[:], fours[:], ends[:, E - 1:E].to_broadcast([P, MG // 4]),
                             ALU.is_lt).then_inc(s_table, 1)
            dve.wait_ge(s_table, 13)
            ev.tensor_reduce(fours_sum[:], fours_used[:], AX.X, ALU.add).then_inc(s_table, 1)
            dve.wait_ge(s_table, 14)
            ev.tensor_scalar(fours_sum[:], fours_sum[:], 1.0, 4.0, ALU.max, ALU.mult).then_inc(s_table, 1)
            dve.wait_ge(s_table, 15)
            ev.tensor_scalar(blocks_more[:], fours_sum[:], -4.0, None, ALU.add).then_inc(s_table, 1)

            dve.wait_ge(s_gate_exp, 1)
            ev.tensor_scalar(gden[:], gexp[:], 1.0, None, ALU.add).then_inc(s_gate, 1)
            dve.wait_ge(s_gate, 1)
            ev.reciprocal(gfirst[:], gden[:]).then_inc(s_gate, 1)
            dve.wait_ge(s_gate, 2)
            ev.tensor_tensor(gates[:, :, 0], gfirst[:], keep[:], ALU.mult).then_inc(s_gate, 1)
            ev.tensor_tensor(gsecond[:], gexp[:], gfirst[:], ALU.mult).then_inc(s_gate, 1)
            dve.wait_ge(s_gate, 4)
            ev.tensor_tensor(gates[:, :, 1], gsecond[:], keep[:], ALU.mult).then_inc(s_gate, 1)
            dve.wait_ge(s_gate, 5)

            def split_rows(i, par):
                dve.wait_ge(s_x32_made, i + 1)
                wait(dve, s_h_made, (i - 1) * CH)
                ev.tensor_copy(xhi[:, par], x32[:]).then_inc(s_x_hi, 1)
                dve.wait_ge(s_x_hi, i + 1)
                ev.tensor_tensor(xlo[:, par], x32[:], xhi[:, par].bitcast(F32), ALU.subtract).then_inc(s_x_lo, 1)

            def copy_yT(i, slot):
                dve.wait_ge(s_y_part, (i + 1) * CH)
                wait(dve, s_yrow_made, i)
                ev.tensor_scalar(yT[:], ps[:, Y_BANKS[slot % 2], :], w2x[:, slot, 2 * HF:2 * HF + 1].bitcast(F32), None,
                                 ALU.add).then_inc(s_yT_made, 1)

            def copy_rows(i, slot):
                dve.wait_ge(s_yrow_made, i + 1)
                wait(dve, res_out[slot], quad(i, slot, 16 * J))
                ev.tensor_copy(yrow[slot].rearrange("p j c -> p (j c)"), ps[:, 6, :]).then_inc(s_yrow_copied, 1)

            def keep_words(i, slot):
                dve.wait_ge(e_in[slot], quad(i, slot, 16) + 16)
                wait(dve, res_out[slot], quad(i, slot, 16 * J))
                ev.tensor_copy(words[:, slot], xg[slot][:, :, C].bitcast(U32)).then_inc(s_words_kept, 1)

            def experts(i, slot):
                par = slot % 2
                for c in range(CH):
                    if c == 3 and has(i - 1):
                        copy_yT(i - 1, (slot - 1) % 4)
                    dve.wait_ge(s_h_hi, i * CH + c + 1)
                    wait(dve, s_y_part, (i - 1) * CH + c + 1)
                    ev.tensor_tensor(hlo[:, c], h32[:, c % 2], hhi[:, c].bitcast(F32), ALU.subtract).then_inc(s_h_lo, 1)
                    if c == 0 and has(i - 2):
                        copy_rows(i - 2, (slot - 2) % 4)
                    if c == 1:
                        split_rows(i + 1, 1 - par)
                keep_words(i + 1, (slot + 1) % 4)

            split_rows(0, 0)
            keep_words(0, 0)
            used = blocks(nc.vector, experts)
            copy_rows(used - 2, 2)
            copy_yT(used - 1, 3)
            copy_rows(used - 1, 3)

            def combine(n, slot):
                par = slot % 2
                dve.wait_ge(f_in[slot], quad(n, slot, 16 * K) + 16 * K)
                for j in range(J):
                    m = ev.scalar_tensor_tensor(half[:, par, j:j + 1], yin[slot][:, 0, j:j + 1],
                                                tile(gates, n, j)[:, 0, 0:1], tile(xres, n, j), ALU.mult, ALU.add)
                m.then_inc(s_f_half, 1)
                dve.wait_ge(s_f_half, n + 1)
                wait(dve, f_out[par], pair(n, par, 16))
                for j in range(J):
                    m = ev.scalar_tensor_tensor(fin[:, par, j:j + 1], yin[slot][:, 1, j:j + 1],
                                                tile(gates, n, j)[:, 0, 1:2], half[:, par, j:j + 1], ALU.mult, ALU.add)
                m.then_inc(s_f_made, 1)

            for n in range(4):
                combine(n, n)
            with nc.vector.Fori(4, NG - 3, 4) as n:
                for d in range(4):
                    combine(n + d, d)

        @block.gpsimd
        def _(pool):
            g = nc.gpsimd
            g.memset(wrouter[:], 0.0).then_inc(s_router_zeroed, 1)
            g.memset(ident[:], 0.0).then_inc(s_ident_set, 1)
            g.memset(in_batch[:], 0.0).then_inc(s_mask_set, 1)
            g.memset(before[:], 1.0).then_inc(s_mask_set, 1)
            g.memset(below[:], 1.0).then_inc(s_mask_set, 1)
            g.memset(ones[:], 1.0)
            g.memset(one[:], 1.0)
            g.memset(filler[:], 1.0)
            g.memset(zeros[:], 0.0).then_inc(s_zeros_set, 1)
            g.iota(expert_no[:], [[1, E]], base=1, channel_multiplier=0, allow_small_or_imprecise_dtypes=True)
            g.iota(fill[:], [[ER, E]], base=0, channel_multiplier=0, allow_small_or_imprecise_dtypes=True)
            g.iota(region_no[:], [[ER, E]], base=0, channel_multiplier=0, allow_small_or_imprecise_dtypes=True)
            g.iota(steps512[:], [[G, NG]], base=0, channel_multiplier=0, allow_small_or_imprecise_dtypes=True)
            g.iota(fours[:], [[4, MG // 4]], base=0, channel_multiplier=0, allow_small_or_imprecise_dtypes=True)
            g.iota(block_no[:], [[1, MG + 1]], base=0, channel_multiplier=0, allow_small_or_imprecise_dtypes=True)
            pool.wait_ge(s_ident_set, 1)
            g.affine_select(ident[:], ident[:], pattern=[[-1, P]], compare_op=ALU.not_equal, fill=1.0, base=0,
                            channel_multiplier=1)
            pool.wait_ge(s_mask_set, 3)
            g.affine_select(in_batch[:], in_batch[:], pattern=[[-T, NB], [-1, T]], compare_op=ALU.is_ge, fill=NEG,
                            base=0, channel_multiplier=1).then_inc(s_batch_mask, 1)
            pool.wait_ge(s_batch_mask, 1)
            g.affine_select(in_batch[:], in_batch[:], pattern=[[-T, NB], [0, T]], compare_op=ALU.is_ge, fill=0.0,
                            base=0, channel_multiplier=1)
            g.affine_select(before[:], before[:], pattern=[[1, P]], compare_op=ALU.is_gt, fill=0.0, base=0,
                            channel_multiplier=-1)
            g.affine_select(below[:], below[:], pattern=[[1, E], [-1, E]], compare_op=ALU.is_ge, fill=0.0, base=0,
                            channel_multiplier=0).then_inc(s_pool_consts, 1)
            g.iota(token[:], [[N, K], [P, J]], base=0, channel_multiplier=1,
                   allow_small_or_imprecise_dtypes=True).then_inc(s_token_next, 1)
            g.memset(pay[:], 0.0).then_inc(s_pay_zeroed, 1)
            g.memset(blank[:], 0.0).then_inc(s_blank_set, 1)
            pool.wait_ge(s_blank_set, 1)
            g.iota(blank_u[:, :, C:C + 1], [[0, J]], base=FAR, channel_multiplier=0).then_inc(s_blank_word, 1)

            def step(t, par):
                odd = 1 - par
                n = t + 2
                if live(n):
                    apart(pool, (s_z1, n + 1))
                    g.tensor_tensor(tiles(xres, n), tiles(xres, n), bo_row[:].unsqueeze(1).to_broadcast([P, J, C]),
                                    ALU.add).then_inc(s_bo_added, 1)
                n = t
                if live(n):
                    apart(pool, (s_p_inv, n + 1),
                                (s_pT_made, n))
                    g.tensor_tensor(pn[:], probs[:], prec[:].unsqueeze(3).to_broadcast([P, H, J, T]),
                                    ALU.mult).then_inc(s_p_norm, 1)
                n = t - 3
                if live(n):
                    apart(pool, (sent[odd], pair(n, odd, SENT)),
                                (s_token_next, n + 1))
                    g.tensor_copy(pay_u[:, odd, :, :, C], token[:]).then_inc(s_word_made, 1)
                    apart(pool, (s_word_made, n + 1))
                    g.tensor_scalar(token[:], token[:], float(G), None, ALU.add).then_inc(s_token_next, 1)
                    apart(pool, (s_route, n * ROUTE + 18),
                                (s_pay_made, n + 1))
                    for k in range(K):
                        for j in range(J):
                            g.indirect_dma_start(rows, bass.IndirectOffsetOnAxis(
                                ap=rows_of[:, odd, k * J + j:k * J + j + 1], axis=0),
                                pay[:, odd, k, j, :], None, bounds_check=E * ER - 1,
                                oob_is_err=False).then_inc(sent[odd], 16)

            pool.wait_ge(s_pay_zeroed, 1)
            pool.wait_ge(s_biases_in, 16 * 4)
            pipeline(nc.gpsimd, step)

            def scatter(i, slot):
                apart(pool, (s_yrow_copied, i + 1))
                for j in range(J):
                    g.indirect_dma_start(results, bass.IndirectOffsetOnAxis(
                        ap=words[:, slot, j:j + 1], axis=0),
                        yrow[slot][:, j, :], None, bounds_check=K * N - 1,
                        oob_is_err=False).then_inc(res_out[slot], 16)

            def experts(i, slot):
                if has(i - 2):
                    scatter(i - 2, (slot - 2) % 4)

            pool.wait_ge(s_results_zeroed, 16 * NG)
            used = blocks(nc.gpsimd, experts)
            scatter(used - 2, 2)
            scatter(used - 1, 3)


_INS = ['r_x', 'r_noise', 'L0_rec_ln1_w', 'L0_rec_ln1_b', 'L0_rec_ln2_w', 'L0_rec_ln2_b', 'L0_rec_Wq', 'L0_rec_Wk',
        'L0_rec_Wv', 'L0_rec_Wo', 'L0_rec_bo', 'L0_rec_Wr', 'L0_rec_br', 'L0_rec_Wn', 'L0_rec_bn', 'L0_rec_Wsk',
        'L0_rec_bsk', 'L0_rec_W1', 'L0_rec_b1', 'L0_rec_W2', 'L0_rec_b2']


def kernel(**inputs):
    import numpy as _np
    import concourse.bacc as _bacc
    from concourse import mybir as _mybir
    from concourse.bass_utils import run_bass_kernel_spmd as _run

    nc = _bacc.Bacc("TRN2", target_bir_lowering=False, num_devices=1)
    arrays, args = {}, []
    for name in _INS:
        a = _np.ascontiguousarray(inputs[name])
        arrays[f"in_{name}"] = a
        args.append(nc.dram_tensor(f"in_{name}", a.shape, _mybir.dt.from_np(a.dtype), kind="ExternalInput").ap())
    out = nc.dram_tensor("out_0", inputs['r_x'].shape, _mybir.dt.float32, kind="ExternalOutput").ap()
    build(nc, *args, out)
    r = _run(nc, [arrays], core_ids=[0])
    return r.results[0]["out_0"]
```
